# Optimizing a Trainium2 kernel written in Bass

```python
import numpy as np
import jax
import jax.numpy as jnp

def _softmax(x, axis=-1):
    return jax.nn.softmax(x, axis=axis)

def _gelu(x):
    return jax.nn.gelu(x, approximate=True)

def _silu(x):
    return jax.nn.silu(x)

def _sigmoid(x):
    return jax.nn.sigmoid(x)

def _layernorm(x, axis=-1, eps=1e-05):
    m = jnp.mean(x, axis=axis, keepdims=True)
    v = jnp.var(x, axis=axis, keepdims=True)
    return (x - m) / jnp.sqrt(v + eps)

def _scatter_add(tgt, idx, src, axis=0):
    return tgt.at[idx].add(src)

def _segment_sum(src, seg, n):
    return jax.ops.segment_sum(src, seg, n)
kernel_name = 'mk_sandwich_d2_jaxref_r8_17b099'

def setup_inputs(seed: int=0):
    np.random.seed(seed)
    _w = jnp.asarray

    def _L0_attn_setup():
        import jax, jax.numpy as jnp
        import numpy as np
        import math
        D_MODEL = 128
        N_HEADS = 16
        LATENT = 32
        key = jax.random.key(seed)
        ks = jax.random.split(key, 9)
        B, T, C, L = (2, 256, D_MODEL, LATENT)
        s = 0.02
        return {'x': jax.random.normal(ks[0], (B, T, C), dtype=jnp.float32), 'Wq': jax.random.normal(ks[1], (C, C), dtype=jnp.float32) * s, 'bq': jnp.zeros((C,), dtype=jnp.float32), 'Wkd': jax.random.normal(ks[2], (C, 2 * L), dtype=jnp.float32) * s, 'bkd': jnp.zeros((2 * L,), dtype=jnp.float32), 'Wku': jax.random.normal(ks[3], (L, 2 * C), dtype=jnp.float32) * s, 'bku': jnp.zeros((2 * C,), dtype=jnp.float32), 'Wo': jax.random.normal(ks[4], (C, C), dtype=jnp.float32) * s, 'bo': jnp.zeros((C,), dtype=jnp.float32)}
    _L0_attn_in = _L0_attn_setup()

    def _L0_ffn_setup():
        import jax, jax.numpy as jnp
        import numpy as np
        TOP_K = 2
        EPS = 1e-05

        def layer_norm(x, g, b):
            mu = jnp.mean(x, axis=-1, keepdims=True)
            var = jnp.mean(jnp.square(x - mu), axis=-1, keepdims=True)
            return (x - mu) * jax.lax.rsqrt(var + EPS) * g + b
        key = jax.random.key(seed)
        ks = jax.random.split(key, 12)
        B, S, D, F, E = (2, 256, 128, 512, 8)
        std = 0.02
        return {'x': jax.random.normal(ks[0], (B, S, D), jnp.float32), 'g1': jnp.ones((D,), jnp.float32), 'be1': jnp.zeros((D,), jnp.float32), 'mix_w': jax.random.normal(ks[1], (D, D), jnp.float32) * std, 'mix_b': jnp.zeros((D,), jnp.float32), 'g2': jnp.ones((D,), jnp.float32), 'be2': jnp.zeros((D,), jnp.float32), 'router_w': jax.random.normal(ks[2], (D, E), jnp.float32) * std, 'w1': jax.random.normal(ks[3], (E, D, F), jnp.float32) * std, 'b1': jnp.zeros((E, F), jnp.float32), 'w2': jax.random.normal(ks[4], (E, F, D), jnp.float32) * std, 'b2': jnp.zeros((E, D), jnp.float32)}
    _L0_ffn_in = _L0_ffn_setup()

    def _L1_attn_setup():
        import jax, jax.numpy as jnp
        import numpy as np
        D_MODEL = 128
        N_HEADS = 16
        HEAD_DIM = D_MODEL // N_HEADS

        def alibi_slopes(n_heads):
            base = 2.0 ** (-8.0 / n_heads)
            return jnp.asarray([base ** i for i in range(1, n_heads + 1)], dtype=jnp.float32)
        key = jax.random.key(seed)
        kx, kq, kk, kv, ko = jax.random.split(key, 5)
        B, T = (2, 256)
        scale = 0.02
        x = jax.random.normal(kx, (B, T, D_MODEL), dtype=jnp.float32)
        Wq = jax.random.normal(kq, (D_MODEL, D_MODEL), dtype=jnp.float32) * scale
        Wk = jax.random.normal(kk, (D_MODEL, D_MODEL), dtype=jnp.float32) * scale
        Wv = jax.random.normal(kv, (D_MODEL, D_MODEL), dtype=jnp.float32) * scale
        Wo = jax.random.normal(ko, (D_MODEL, D_MODEL), dtype=jnp.float32) * scale
        return {'x': x, 'Wq': Wq, 'Wk': Wk, 'Wv': Wv, 'Wo': Wo}
    _L1_attn_in = _L1_attn_setup()

    def _L1_ffn_setup():
        import jax, jax.numpy as jnp
        import numpy as np
        B, S, D, E, F = (2, 128, 128, 14, 256)
        key = jax.random.key(seed)
        k0, k1, k2, k3 = jax.random.split(key, 4)
        h = jax.random.normal(k0, (B, S, D), jnp.float32)
        gate_w = jax.random.normal(k1, (E, D), jnp.float32) * 0.02
        w1 = jax.random.normal(k2, (E, D, F), jnp.float32) * (1.0 / np.sqrt(D).astype(np.float32))
        b1 = jnp.zeros((E, F), jnp.float32)
        w2 = jax.random.normal(k3, (E, F, D), jnp.float32) * (1.0 / np.sqrt(F).astype(np.float32))
        b2 = jnp.zeros((E, D), jnp.float32)
        return {'h': h, 'gate_w': gate_w, 'w1': w1, 'b1': b1, 'w2': w2, 'b2': b2}
    _L1_ffn_in = _L1_ffn_setup()
    _d = {'L0_attn_x': _L0_attn_in['x'], 'L0_attn_Wq': _L0_attn_in['Wq'], 'L0_attn_bq': _L0_attn_in['bq'], 'L0_attn_Wkd': _L0_attn_in['Wkd'], 'L0_attn_bkd': _L0_attn_in['bkd'], 'L0_attn_Wku': _L0_attn_in['Wku'], 'L0_attn_bku': _L0_attn_in['bku'], 'L0_attn_Wo': _L0_attn_in['Wo'], 'L0_attn_bo': _L0_attn_in['bo'], 'L0_ffn_g1': _L0_ffn_in['g1'], 'L0_ffn_be1': _L0_ffn_in['be1'], 'L0_ffn_mix_w': _L0_ffn_in['mix_w'], 'L0_ffn_mix_b': _L0_ffn_in['mix_b'], 'L0_ffn_g2': _L0_ffn_in['g2'], 'L0_ffn_be2': _L0_ffn_in['be2'], 'L0_ffn_router_w': _L0_ffn_in['router_w'], 'L0_ffn_w1': _L0_ffn_in['w1'], 'L0_ffn_b1': _L0_ffn_in['b1'], 'L0_ffn_w2': _L0_ffn_in['w2'], 'L0_ffn_b2': _L0_ffn_in['b2'], 'L1_attn_Wq': _L1_attn_in['Wq'], 'L1_attn_Wk': _L1_attn_in['Wk'], 'L1_attn_Wv': _L1_attn_in['Wv'], 'L1_attn_Wo': _L1_attn_in['Wo'], 'L1_ffn_gate_w': _L1_ffn_in['gate_w'], 'L1_ffn_w1': _L1_ffn_in['w1'], 'L1_ffn_b1': _L1_ffn_in['b1'], 'L1_ffn_w2': _L1_ffn_in['w2'], 'L1_ffn_b2': _L1_ffn_in['b2']}
    _x0 = _d['L0_attn_x']
    _d['L0_attn_x'] = jax.random.normal(jax.random.fold_in(jax.random.key(seed), 1), (16, 512, 128), dtype=_x0.dtype)
    del _x0
    return _d

def reference(L0_attn_x, L0_attn_Wq, L0_attn_bq, L0_attn_Wkd, L0_attn_bkd, L0_attn_Wku, L0_attn_bku, L0_attn_Wo, L0_attn_bo, L0_ffn_g1, L0_ffn_be1, L0_ffn_mix_w, L0_ffn_mix_b, L0_ffn_g2, L0_ffn_be2, L0_ffn_router_w, L0_ffn_w1, L0_ffn_b1, L0_ffn_w2, L0_ffn_b2, L1_attn_Wq, L1_attn_Wk, L1_attn_Wv, L1_attn_Wo, L1_ffn_gate_w, L1_ffn_w1, L1_ffn_b1, L1_ffn_w2, L1_ffn_b2):

    def _L0_attn_ref(x, Wq, bq, Wkd, bkd, Wku, bku, Wo, bo):
        import jax, jax.numpy as jnp
        import numpy as np
        import math
        D_MODEL = 128
        N_HEADS = 16
        LATENT = 32
        B, T, C = x.shape
        H = N_HEADS
        D = C // H
        L = LATENT
        q = (x @ Wq + bq).reshape(B, T, H, D)
        kv_latent = jax.nn.gelu(x @ Wkd + bkd, approximate=False)
        lat = kv_latent[..., :L] + kv_latent[..., L:]
        kv = lat @ Wku + bku
        k = kv[..., :C].reshape(B, T, H, D)
        v = kv[..., C:].reshape(B, T, H, D)
        scale = 1.0 / math.sqrt(D)
        attn = jnp.einsum('bqhd,bkhd->bhqk', q, k) * scale
        causal = jnp.tril(jnp.ones((T, T), dtype=bool))
        attn = jnp.where(causal, attn, -jnp.inf)
        attn = jax.nn.softmax(attn, axis=-1)
        out = jnp.einsum('bhqk,bkhd->bqhd', attn, v).reshape(B, T, C)
        return out @ Wo + bo

    def _L0_ffn_ref(x, g1, be1, mix_w, mix_b, g2, be2, router_w, w1, b1, w2, b2):
        import jax, jax.numpy as jnp
        import numpy as np
        TOP_K = 2
        EPS = 1e-05

        def layer_norm(x, g, b):
            mu = jnp.mean(x, axis=-1, keepdims=True)
            var = jnp.mean(jnp.square(x - mu), axis=-1, keepdims=True)
            return (x - mu) * jax.lax.rsqrt(var + EPS) * g + b
        res = x
        n = layer_norm(x, g1, be1)
        x = res + n + (n @ mix_w + mix_b)
        res = x
        n = layer_norm(x, g2, be2)
        B, S, D = n.shape
        E = w1.shape[0]
        flat = n.reshape(-1, D)
        probs = jax.nn.softmax(flat @ router_w, axis=-1)
        topw, topi = jax.lax.top_k(probs, TOP_K)
        combine = jnp.sum(jax.nn.one_hot(topi, E, dtype=flat.dtype) * topw[..., None], axis=1)
        h = jax.nn.silu(jnp.einsum('td,edf->tef', flat, w1) + b1)
        y = jnp.einsum('tef,efd->ted', h, w2) + b2
        out = jnp.einsum('te,ted->td', combine, y)
        return res + out.reshape(B, S, D)

    def _L1_attn_ref(x, Wq, Wk, Wv, Wo):
        import jax, jax.numpy as jnp
        import numpy as np
        D_MODEL = 128
        N_HEADS = 16
        HEAD_DIM = D_MODEL // N_HEADS

        def alibi_slopes(n_heads):
            base = 2.0 ** (-8.0 / n_heads)
            return jnp.asarray([base ** i for i in range(1, n_heads + 1)], dtype=jnp.float32)
        B, T, D = x.shape
        H, hd = (N_HEADS, HEAD_DIM)

        def proj(W):
            return (x @ W.T).reshape(B, T, H, hd).transpose(0, 2, 1, 3)
        q, k, v = (proj(Wq), proj(Wk), proj(Wv))
        scale = hd ** (-0.5)
        scores = jnp.einsum('bhqd,bhkd->bhqk', q, k) * scale
        pos = jnp.arange(T, dtype=jnp.float32)
        dist = jnp.abs(pos[:, None] - pos[None, :])
        causal = pos[:, None] >= pos[None, :]
        slopes = alibi_slopes(H)
        bias = -slopes[:, None, None] * jnp.where(causal, dist, 0.0)
        scores = scores + bias[None]
        scores = jnp.where(causal[None, None], scores, -jnp.inf)
        attn = jax.nn.softmax(scores, axis=-1)
        out = jnp.einsum('bhqk,bhkd->bhqd', attn, v)
        out = out.transpose(0, 2, 1, 3).reshape(B, T, D)
        return out @ Wo.T

    def _L1_ffn_ref(h, gate_w, w1, b1, w2, b2):
        import jax, jax.numpy as jnp
        import numpy as np
        B, S, D, E, F = (2, 128, 128, 14, 256)
        Bb, Ss, Dd = h.shape
        x = h.reshape(Bb * Ss, Dd)
        logits = x @ gate_w.T
        probs = jax.nn.softmax(logits, axis=-1)
        top2_p, top2_i = jax.lax.top_k(probs, 2)
        w = top2_p / jnp.maximum(top2_p.sum(-1, keepdims=True), 1e-10)
        hh = jnp.einsum('nd,edf->nef', x, w1) + b1
        hh = jax.nn.gelu(hh, approximate=False)
        all_out = jnp.einsum('nef,efd->ned', hh, w2) + b2
        n = jnp.arange(x.shape[0])
        out0 = all_out[n, top2_i[:, 0]]
        out1 = all_out[n, top2_i[:, 1]]
        moe_out = w[:, 0:1] * out0 + w[:, 1:2] * out1
        result = jnp.clip(x + moe_out, -100.0, 100.0).reshape(Bb, Ss, Dd)
        return result
    x = L0_attn_x
    x = x + _layernorm(_L0_attn_ref(_layernorm(x, axis=-1), L0_attn_Wq, L0_attn_bq, L0_attn_Wkd, L0_attn_bkd, L0_attn_Wku, L0_attn_bku, L0_attn_Wo, L0_attn_bo), axis=-1)
    x = x + _layernorm(_L0_ffn_ref(_layernorm(x, axis=-1), L0_ffn_g1, L0_ffn_be1, L0_ffn_mix_w, L0_ffn_mix_b, L0_ffn_g2, L0_ffn_be2, L0_ffn_router_w, L0_ffn_w1, L0_ffn_b1, L0_ffn_w2, L0_ffn_b2), axis=-1)
    x = x + _layernorm(_L1_attn_ref(_layernorm(x, axis=-1), L1_attn_Wq, L1_attn_Wk, L1_attn_Wv, L1_attn_Wo), axis=-1)
    x = x + _layernorm(_L1_ffn_ref(_layernorm(x, axis=-1), L1_ffn_gate_w, L1_ffn_w1, L1_ffn_b1, L1_ffn_w2, L1_ffn_b2), axis=-1)
    return x

_drawn_inputs = setup_inputs


def setup_inputs(seed=0):
    import zlib

    import numpy as np

    out = dict(_drawn_inputs(seed))
    spreads = {'L0_attn_bq': (0.0, 0.8),
     'L0_attn_bkd': (0.0, 0.455),
     'L0_attn_bku': (0.0, 0.1),
     'L0_attn_bo': (0.0, 0.1),
     'L0_ffn_g1': (1.0, 0.2),
     'L0_ffn_be1': (0.0, 0.1),
     'L0_ffn_mix_b': (0.0, 0.272),
     'L0_ffn_g2': (1.0, 0.6),
     'L0_ffn_be2': (0.0, 0.8),
     'L0_ffn_b1': (0.0, 0.8),
     'L0_ffn_b2': (0.0, 0.8),
     'L1_ffn_b1': (0.0, 0.635),
     'L1_ffn_b2': (0.0, 0.466)}
    factors = {'L0_attn_Wq': 8.0,
     'L0_attn_Wkd': 7.771,
     'L0_attn_Wku': 3.414,
     'L0_ffn_router_w': 6.727,
     'L0_ffn_w1': 8.0,
     'L0_ffn_w2': 8.0,
     'L1_attn_Wq': 8.0,
     'L1_attn_Wk': 8.0}
    for name, (base, spread) in spreads.items():
        noise = np.random.default_rng([zlib.crc32(name.encode()), seed]).standard_normal(out[name].shape)
        drawn = base * np.exp(spread * noise) if base else spread * noise
        out[name] = jnp.asarray(drawn.astype(out[name].dtype))
    for name, factor in factors.items():
        out[name] = (out[name] * factor).astype(out[name].dtype)
    return out
```

```python
from contextlib import ExitStack
import concourse.bass as bass
from concourse import mybir

F32 = mybir.dt.float32
BF16 = mybir.dt.bfloat16
I32 = mybir.dt.int32
U32 = mybir.dt.uint32
ALU = mybir.AluOpType
ACT = mybir.ActivationFunctionType
AX = mybir.AxisListType.X

P = 128
B, T, C = 16, 512, 128
H, D = 16, 8
TT = T // P
PAIRS = H // 2
SCALE = D ** -0.5
EPS = 1e-5
NB = 3
TERMS = 6
ALIBI_ROW = TERMS * D
MAX_ROW = ALIBI_ROW + 3
SLOTS = TT * (H // 4)
GROUPS = 2 * SLOTS
MAX_GROUPS = [(qt, h0, n) for qt, n in ((0, 4), (1, 2), (2, 1), (3, 1)) for h0 in range(0, 8, n)]
MG = len(MAX_GROUPS)
MAX_PER_SLOT = [3, 3, 3, 3, 3, 3, 2, 2]
NEG = -1e30
LOADS = 16 * 4
WRITES = 16 * 3


def has(b):
    return not isinstance(b, int) or 0 <= b < B


def begun(count):
    return not isinstance(count, int) or count > 0


class Attention:

    def __init__(self, stack, ctx, nc, x_sb):
        def sb(name, shape, dt=F32):
            return stack.enter_context(nc.sbuf_tensor(name, shape, dt))

        def sem(name):
            return ctx.enter_context(nc.semaphore(name))

        self.x = x_sb
        self.q_stack = sb("q_stack", [P, NB, PAIRS, T], BF16)
        self.k_stack = sb("k_stack", [P, NB, 2, PAIRS, T], BF16)
        self.v_aug = sb("v_aug", [P, NB, TT, H, 32])
        self.probs = sb("probs", [P, 4, 2, T])
        self.xn = sb("xn", [P, TT, C])
        self.xn_t = sb("xn_t", [P, T])
        self.gelu = sb("gelu", [64, T])
        self.part = sb("part", [P, 2, 3, T], BF16)
        self.full = sb("full", [P, 2, T])
        self.rest = sb("rest", [P, T])
        self.neg_max = sb("neg_max", [P, 2, TT, 8])
        self.max_rest = sb("max_rest", [P, TT, 8])
        self.max_part = sb("max_part", [P, 2, TT, 3, 8], BF16)
        self.max_t = sb("max_t", [24, 2, T], BF16)
        self.quad = sb("quad", [P, T])
        self.recip = sb("recip", [P, TT, 4])
        self.heads_out = sb("heads_out", [P, TT, H, D])
        self.heads_t = sb("heads_t", [P, T])
        self.y = sb("y", [P, TT, C])
        self.stats = sb("stats", [P, 2, TT, 6])
        self.mean_var = sb("mean_var", [P, 2, TT, 2])
        self.rstd = sb("rstd", [P, 2, TT])
        (self.xn_stats, self.xn_var, self.xn_rstd, self.xn_ready, self.xnt_full, self.xnt_ready) = (sem(name) for name in
            "xn_stats xn_var xn_rstd xn_ready xnt_full xnt_ready".split())
        (self.gelu_full, self.gelu_ready, self.q_full, self.q_ready, self.k_full, self.k_ready) = (sem(name) for name in
            "gelu_full gelu_ready q_full q_ready k_full k_ready".split())
        (self.rest_ready, self.mid_ready, self.parts_ready, self.v_full, self.v_ready,
         self.parts_written) = (sem(name) for name in
            "rest_ready mid_ready parts_ready v_full v_ready parts_written".split())
        (self.stack_loaded, self.max_full, self.max_taken, self.max_step, self.max_parts,
         self.maxt_full) = (sem(name) for name in
            "stack_loaded max_full max_taken max_step max_parts maxt_full".split())
        (self.maxt_ready, self.max_written, self.max_loaded, self.scores_full, self.probs_ready,
         self.pv_done) = (sem(name) for name in
            "maxt_ready max_written max_loaded scores_full probs_ready pv_done".split())
        (self.quad_ready, self.outt_full, self.out_recip, self.out_ready, self.headst_full,
         self.headst_ready) = (sem(name) for name in
            "quad_ready outt_full out_recip out_ready headst_full headst_ready".split())
        (self.y_full, self.y_ready, self.y_stats, self.y_var, self.y_rstd, self.y_normed) = (sem(name) for name in
            "y_full y_ready y_stats y_var y_rstd y_normed".split())
        (self.x_ready, self.xn_eps, self.y_eps, self.v_zeroed, self.rows_set, self.rows_written) = (sem(name) for name in
            "x_ready xn_eps y_eps v_zeroed rows_set rows_written".split())


def max_schedule():
    order = [(ph, g) for ph in range(2) for g in range(MG)]
    out = []
    for n in MAX_PER_SLOT * 2:
        out.append(order[:n])
        order = order[n:]
    assert not order
    return out




def sweep(eng, body, first):
    lo, hi = 4, B - 3
    for n in range(first, lo):
        body(n, n % NB)
    with eng.Fori(0, (hi - lo) // NB) as i:
        for u in range(NB):
            body(i * NB + (lo + u), (lo + u) % NB)
    for n in range(hi, B + 3):
        body(n, n % NB)


def attention_tensor(pe, nc, A, W, R, Q=None):
    mm, tr = nc.tensor.matmul, nc.tensor.transpose
    layer = R.layer
    first = layer * B
    schedule = max_schedule()
    misc16 = W.misc[:, :].bitcast(BF16)

    def body(n, turn):
        now = n + first
        cur, nxt, new = turn, (turn + 1) % NB, (turn + 2) % NB
        if has(n - 3):
            free = (R.ranks_taken, n - 2)
        elif n >= 1:
            free = (A.out_ready, TT * now - 1)
        else:
            free = (A.v_ready, now + 2) if n > -2 else None

        def misc_is_free():
            if free:
                pe.wait_ge(*free)

        def scores(slot, half_of_quad):
            j, kt = divmod(slot, TT)
            pair, g = 2 * j + half_of_quad, 2 * slot + half_of_quad
            if slot == 0 and half_of_quad == 0:
                pe.wait_ge(A.max_loaded, 64 * now + 32)
            if slot == SLOTS // 2 and half_of_quad == 0:
                pe.wait_ge(A.max_loaded, 64 * now + 64)
            if begun(GROUPS * now + g - 1):
                pe.wait_ge(A.probs_ready, GROUPS * now + g - 1)
            for half in range(2):
                bank = W.s_ps[:, 2 * (g % 2) + half, :]
                mm(bank[:, 0:P], W.causal[:, :], W.ident16[:, :], start=True, stop=False,
                   skip_group_check=True)
                last = mm(bank[:, 0:T - kt * P],
                          A.k_stack[:, cur, half, pair, kt * P:(kt + 1) * P],
                          A.q_stack[:, cur, pair, kt * P:T], start=False, stop=True, skip_group_check=True)
            last.then_inc(A.scores_full, 1)

        def weigh(slot, at, buf):
            j, kt = divmod(slot, TT)
            if kt == 0:
                if begun(TT * at + j):
                    pe.wait_ge(A.quad_ready, TT * at + j)
            for i in range(2):
                g = 2 * slot + i
                pe.wait_ge(A.probs_ready, GROUPS * at + g + 1)
                for half in range(2):
                    c = 2 * i + half
                    last = mm(W.o_ps[32 * c:32 * c + 32, kt * P:T],
                              A.v_aug[:, buf, kt, 4 * j + c, :],
                              A.probs[:, g % 4, half, 0:T - kt * P],
                              start=(kt == 0), stop=(kt == TT - 1))
                last.then_inc(A.pv_done, 1)

        def max_group(ph, g):
            qt, h0, heads = MAX_GROUPS[g]
            if ph == 0 and g == 0:
                pe.wait_ge(A.stack_loaded, LOADS * (now + 2))
            count = 2 * MG * (now + 1) + ph * MG + g
            if begun(count - 1):
                pe.wait_ge(A.max_taken, count - 1)
            keys = (qt + 1) * P
            bank = W.m_ps[:, g % 2, 0:heads * keys].rearrange("p (h k) -> p h k", h=heads)
            mm(bank[:, :, keys - P:keys], W.ident16[:, :],
               W.causal[:, :].unsqueeze(1).to_broadcast([P, heads, P]), start=True, stop=False,
               skip_group_check=True)
            for h in range(h0, h0 + heads):
                half, pair = h // 4, 4 * ph + h % 4
                last = mm(bank[:, h - h0, :], A.q_stack[:, nxt, pair, qt * P:(qt + 1) * P],
                          A.k_stack[:, nxt, half, pair, 0:keys], start=False,
                          stop=(h == h0 + heads - 1), skip_group_check=True)
            last.then_inc(A.max_full, 1)

        def max_turned(ph, at):
            misc_is_free()
            pe.wait_ge(A.max_parts, 2 * at + ph + 1)
            for qt in range(TT):
                last = tr(misc16[0:24, qt * P:(qt + 1) * P],
                          A.max_part[:, ph, qt, :, :].rearrange("p a b -> p (a b)"), W.ident16[:, :])
            last.then_inc(A.maxt_full, 1)
            return A.maxt_ready, 2 * at + ph + 1

        def heads_turned(j, at):
            misc_is_free()
            pe.wait_ge(A.quad_ready, TT * at + j + 1)
            for t in range(TT):
                last = tr(W.misc[:, t * P:(t + 1) * P], A.quad[:, t * P:(t + 1) * P], W.ident[:, :])
            last.then_inc(A.outt_full, 1)
            return A.out_ready, TT * at + j + 1

        def project_x():
            misc_is_free()
            pe.wait_ge(A.xn_ready, now + 3)
            for t in range(TT):
                last = tr(W.misc[:, t * P:(t + 1) * P], A.xn[:, t, :], W.ident[:, :])
            last.then_inc(A.xnt_full, 1)
            return A.xnt_ready, now + 3

        def project_latent():
            misc_is_free()
            pe.wait_ge(A.xnt_ready, now + 3)
            mm(W.misc[0:64, :], W.wkd[:, :], A.xn_t[:, :], start=True, stop=True).then_inc(A.gelu_full, 1)
            return A.gelu_ready, now + 3

        def project_q():
            misc_is_free()
            pe.wait_ge(A.xnt_ready, now + 3)
            mm(W.misc[:, :], W.wq[layer][:, :], A.xn_t[:, :], start=True, stop=True).then_inc(A.q_full, 1)
            return A.q_ready, now + 3

        def project_k():
            misc_is_free()
            if layer == 0:
                pe.wait_ge(A.gelu_ready, now + 3)
                last = mm(W.misc[:, :], W.wku[:, 0:C], A.gelu[:, :], start=True, stop=True)
            else:
                last = mm(W.misc[:, :], W.wk1[:, :], A.xn_t[:, :], start=True, stop=True)
            last.then_inc(A.k_full, 1)
            return A.k_ready, now + 3

        def project_v():
            misc_is_free()
            for t in range(TT):
                rows = slice(t * P, (t + 1) * P)
                if layer == 0:
                    last = mm(W.misc[:, rows], A.gelu[:, rows], W.wku[:, C:2 * C], start=True, stop=True)
                else:
                    last = mm(W.misc[:, rows], A.xn_t[:, rows], W.wv1[:, :], start=True, stop=True)
            last.then_inc(A.v_full, 1)
            return A.v_ready, now + 3

        def finish_turned():
            misc_is_free()
            pe.wait_ge(A.out_ready, TT * now)
            for t in range(TT):
                last = tr(W.misc[:, t * P:(t + 1) * P],
                          A.heads_out[:, t, :, :].rearrange("p h d -> p (h d)"), W.ident[:, :])
            last.then_inc(A.headst_full, 1)
            return A.headst_ready, now

        def finish_y():
            misc_is_free()
            pe.wait_ge(A.headst_ready, now)
            for t in range(TT):
                rows = slice(t * P, (t + 1) * P)
                last = mm(W.misc[:, rows], A.heads_t[:, rows], W.wo[layer][:, :], start=True, stop=True)
            last.then_inc(A.y_full, 1)
            return A.y_ready, now

        for slot in range(SLOTS):
            groups = schedule[slot] if has(n + 1) else []
            if has(n):
                scores(slot, 0)
            for ph, g in groups[:1]:
                max_group(ph, g)
            if slot == 6 and has(n - 2) and layer == 0:
                misc_is_free()
                free = route_turn_n(pe, nc, R, W, n - 2)
            if slot == 8 and has(n - 2) and layer == 0:
                misc_is_free()
                free = route_mix(pe, nc, R, W, n - 2)
            if slot == 5 and has(n - 1):
                free = finish_turned()
            if has(n):
                scores(slot, 1)
            for ph, g in groups[1:2]:
                max_group(ph, g)
            if slot == 0 and has(n - 1):
                weigh(SLOTS - 1, now - 1, (cur - 1) % NB)
            if slot > 0 and has(n):
                weigh(slot - 1, now, cur)
            for ph, g in groups[2:]:
                max_group(ph, g)
            if slot == 0 and has(n):
                free = max_turned(1, now)
            if slot == 1 and has(n - 1):
                free = heads_turned(3, now - 1)
            if slot == 2 and has(n + 2):
                free = project_x()
            if slot == 3 and has(n + 2) and layer == 0:
                free = project_latent()
            if slot == 4 and has(n + 2):
                free = project_q()
            if slot == 5 and has(n + 2):
                free = project_k()
            if slot in (6, 10, 14) and has(n):
                free = heads_turned({6: 0, 10: 1, 14: 2}[slot], now)
            if slot == 8 and has(n - 1):
                free = finish_y()
            if slot == 9 and has(n + 1):
                free = max_turned(0, now + 1)
            if slot == 11 and has(n + 2):
                free = project_v()
            if slot == 12 and has(n - 2):
                misc_is_free()
                free = route_turn_rows(pe, nc, R, W, n - 2, nxt)
            if slot == 13 and has(n - 2):
                misc_is_free()
                free = route_logits(pe, nc, R, W, n - 2)
            if slot == 15 and has(n - 2):
                misc_is_free()
                free = route_ranks(pe, nc, R, W, n - 2)

    pe.wait_ge(A.rows_set, layer + 1)
    sweep(pe, body, -2 if layer == 0 else -3)


def attention_scalar(act, nc, A, W, R, Q=None):
    do = nc.scalar.activation
    layer = R.layer
    first = layer * B

    def body(n, turn):
        now = n + first

        def exps(slot, i):
            kt, g = slot % TT, 2 * slot + i
            act.wait_ge(A.scores_full, GROUPS * now + g + 1)
            if begun(GROUPS * now + g - 3):
                act.wait_ge(A.pv_done, GROUPS * now + g - 3)
            do(A.probs[:, g % 4, :, 0:T - kt * P], W.s_ps[:, 2 * (g % 2):2 * (g % 2) + 2, 0:T - kt * P],
               ACT.Exp, scale=SCALE).then_inc(A.probs_ready, 1)

        def take_quad(j, at):
            act.wait_ge(A.pv_done, GROUPS * at + 8 * (j + 1))
            if begun(TT * at + j):
                act.wait_ge(A.outt_full, TT * at + j)
            do(A.quad[:, :], W.o_ps[:, :], ACT.Copy).then_inc(A.quad_ready, 1)

        def take_parts(which, bias, full, ready):
            act.wait_ge(full, now + 3)
            if begun(2 * (now + 2)):
                act.wait_ge(A.parts_ready, 2 * (now + 2))
            if begun(2 * WRITES * (now + 2)):
                act.wait_ge(A.parts_written, 2 * WRITES * (now + 2))
            if bias is None:
                do(A.full[:, which, :], W.misc[:, :], ACT.Copy)
                do(A.part[:, which, 0, :], W.misc[:, :], ACT.Copy).then_inc(ready, 1)
            else:
                do(A.full[:, which, :], W.misc[:, :], ACT.Identity, bias=bias)
                do(A.part[:, which, 0, :], W.misc[:, :], ACT.Identity, bias=bias).then_inc(ready, 1)

        for slot in range(SLOTS):
            if has(n):
                exps(slot, 0)
            if slot == 3 and has(n + 2):
                act.wait_ge(A.xnt_full, now + 3)
                if begun(now + 2):
                    act.wait_ge(A.v_full, now + 2)
                do(A.xn_t[:, :], W.misc[:, :], ACT.Copy).then_inc(A.xnt_ready, 1)
            if slot == 4 and has(n + 2) and layer == 0:
                act.wait_ge(A.gelu_full, now + 3)
                do(A.gelu[:, :], W.misc[0:64, :], ACT.Gelu, bias=W.bkd[:, :]).then_inc(A.gelu_ready, 1)
            if slot == 5 and has(n + 2):
                take_parts(0, W.bq[:, :] if layer == 0 else None, A.q_full, A.q_ready)
            if slot == 6 and has(n + 2):
                take_parts(1, W.bk[:, :] if layer == 0 else None, A.k_full, A.k_ready)
            if slot == 13 and has(n - 2):
                route_scalar_rows(act, nc, R, W, n - 2)
            if has(n):
                exps(slot, 1)
            if slot == 6 and has(n - 2) and layer == 0:
                route_scalar_n(act, nc, R, W, n - 2)
            if slot == 14 and has(n - 2):
                route_scalar_exp(act, nc, R, W, n - 2)
            if slot == 0 and has(n - 1):
                take_quad(3, now - 1)
            if slot == 5 and has(n - 1):
                act.wait_ge(A.headst_full, now)
                do(A.heads_t[:, :], W.misc[:, :], ACT.Copy).then_inc(A.headst_ready, 1)
            if slot in (4, 8, 12) and has(n):
                take_quad(slot // 4 - 1, now)

    sweep(act, body, -2 if layer == 0 else -3)


def attention_vector(dve, nc, A, W, R, Q=None):
    v = nc.vector
    layer = R.layer
    first = layer * B
    schedule = max_schedule()

    def body(n, turn):
        now = n + first
        cur, nxt, new = turn, (turn + 1) % NB, (turn + 2) % NB

        def take_max(ph, g):
            qt, h0, heads = MAX_GROUPS[g]
            if g == 0:
                if begun(2 * now + ph + 1):
                    dve.wait_ge(A.max_parts, 2 * now + ph + 1)
            dve.wait_ge(A.max_full, 2 * MG * (now + 1) + ph * MG + g + 1)
            v.tensor_reduce(A.neg_max[:, ph, qt, h0:h0 + heads],
                            W.m_ps[:, g % 2, 0:heads * (qt + 1) * P].rearrange("p (h k) -> p h k", h=heads),
                            AX.X, ALU.max, negate=True).then_inc(A.max_taken, 1)

        def split_max(ph):
            src, part, rest = A.neg_max[:, ph, :, :], A.max_part[:, ph], A.max_rest[:, :, :]
            steps = 3 * (2 * (now + 1) + ph)
            dve.wait_ge(A.max_taken, 2 * MG * (now + 1) + (ph + 1) * MG)
            if begun(2 * now + ph + 1):
                dve.wait_ge(A.maxt_full, 2 * now + ph + 1)
            v.tensor_copy(part[:, :, 0, :], src).then_inc(A.max_step, 1)
            dve.wait_ge(A.max_step, steps + 1)
            v.tensor_tensor(rest, src, part[:, :, 0, :], ALU.subtract).then_inc(A.max_step, 1)
            dve.wait_ge(A.max_step, steps + 2)
            v.tensor_copy(part[:, :, 1, :], rest).then_inc(A.max_step, 1)
            dve.wait_ge(A.max_step, steps + 3)
            v.tensor_tensor(part[:, :, 2, :], rest, part[:, :, 1, :], ALU.subtract).then_inc(A.max_parts, 1)

        def take_turned_max(ph, at):
            dve.wait_ge(A.maxt_full, 2 * at + ph + 1)
            if begun(16 * (2 * (at - 1) + ph + 1)):
                dve.wait_ge(A.max_written, 16 * (2 * (at - 1) + ph + 1))
            v.tensor_copy(A.max_t[:, ph, :], W.misc[0:24, 0:T // 2].bitcast(BF16)).then_inc(A.maxt_ready, 1)

        def take_heads(j, at):
            quad = W.misc[:, :].rearrange("p (t h c) -> p t h c", t=TT, h=4)
            dve.wait_ge(A.outt_full, TT * at + j + 1)
            if j == 0:
                if begun(at):
                    dve.wait_ge(A.headst_full, at)
            v.reciprocal(A.recip[:, :, :], quad[:, :, :, D]).then_inc(A.out_recip, 1)
            dve.wait_ge(A.out_recip, TT * at + j + 1)
            v.tensor_tensor(A.heads_out[:, :, 4 * j:4 * j + 4, :], quad[:, :, :, 0:D],
                            A.recip[:, :, :].unsqueeze(3).to_broadcast([P, TT, 4, D]),
                            ALU.mult).then_inc(A.out_ready, 1)

        def mean_var(src, k, stats_sem, var_sem, count):
            for t in range(TT):
                last = v.bn_stats(A.stats[:, k, t, :], src(t))
            last.then_inc(stats_sem, 1)
            dve.wait_ge(stats_sem, count)
            dve.sem_inc(W.passed, 1)
            for t in range(TT):
                last = v.bn_aggr(A.mean_var[:, k, t, :], A.stats[:, k, t, :])
            last.then_inc(var_sem, 1)

        def normalise(dst, src, k, sem):
            for t in range(TT):
                last = v.tensor_scalar(dst[:, t, :], src(t), A.mean_var[:, k, t, 0:1],
                                       A.rstd[:, k, t:t + 1], ALU.subtract, ALU.mult)
            last.then_inc(sem, 1)

        def x_in(t):
            return A.x[:, (n + 2) * TT + t, :]

        for slot in range(SLOTS):
            if slot == 0 and has(n + 3) and layer == 1:
                collect_index(dve, nc, Q, n + 3, turn)
            if slot == 0 and has(n - 3):
                route.take_ranks(n - 3)
            if has(n + 1):
                for ph, g in schedule[slot]:
                    take_max(ph, g)
            if slot == 0 and has(n - 2):
                route.x_stats(n - 2)
            if slot == 1 and has(n - 2):
                route.x_norm(n - 2, nxt)
            if slot == 2 and has(n - 2) and layer == 0:
                route.second_norm(n - 2)
            if slot == 2 and has(n - 3):
                route.place(n - 3, cur)
            if slot == 8 and has(n - 2) and layer == 0:
                route.mixed(n - 2)
            if slot == 9 and has(n - 2) and layer == 0:
                route.third_norm(n - 2)
            if slot == 12 and has(n + 3) and layer == 1:
                collect_sum(dve, nc, Q, W, n + 3)
            if slot == 14 and has(n - 2):
                route.logits(n - 2)
            if slot == 14 and has(n + 3) and layer == 1:
                collect_add(dve, nc, Q, A, n + 3)
            if slot == 15 and has(n - 2):
                route.choose(n - 2)
            if slot == 0 and has(n):
                take_turned_max(1, now)
            if slot == 1 and has(n - 1):
                take_heads(3, now - 1)
            if slot == 0 and has(n + 2):
                W.wait_for_x(dve, layer, n + 2)
                if begun(now + 2):
                    dve.wait_ge(A.xn_rstd, now + 2)
                    dve.sem_inc(W.passed, 1)
                mean_var(x_in, 0, A.xn_stats, A.xn_var, now + 3)
            if slot == 1 and has(n + 2):
                dve.wait_ge(A.xn_rstd, now + 3)
                if begun(now + 2):
                    dve.wait_ge(A.xnt_full, now + 2)
                normalise(A.xn, x_in, 0, A.xn_ready)
            if slot == 8 and has(n - 1):
                dve.wait_ge(A.y_full, now)
                if begun(now - 1):
                    dve.wait_ge(A.x_ready, now - 1)
                misc = W.misc[:, :].rearrange("p (t c) -> p t c", t=TT)
                if layer == 0:
                    v.tensor_tensor(A.y[:, :, :], misc, W.bo[:, :].unsqueeze(1).to_broadcast([P, TT, C]),
                                    ALU.add).then_inc(A.y_ready, 1)
                else:
                    v.tensor_copy(A.y[:, :, :], misc).then_inc(A.y_ready, 1)
                dve.wait_ge(A.y_ready, now)
                mean_var(lambda t: A.y[:, t, :], 1, A.y_stats, A.y_var, now)
            if slot == 9 and has(n - 1):
                dve.wait_ge(A.y_rstd, now)
                normalise(A.y, lambda t: A.y[:, t, :], 1, A.y_normed)
                dve.wait_ge(A.y_normed, now)
                rows = A.x[:, bass.ds((n - 1) * TT, TT), :]
                v.tensor_tensor(rows, rows, A.y[:, :, :], ALU.add).then_inc(A.x_ready, 1)
            if slot in (6, 8) and has(n + 2):
                which = 0 if slot == 6 else 1
                dve.wait_ge(A.rest_ready, 2 * (now + 2) + which + 1)
                v.tensor_copy(A.part[:, which, 1, :], A.rest[:, :]).then_inc(A.mid_ready, 1)
            if slot == 7 and has(n + 1):
                split_max(0)
            if slot == 9 and has(n + 1):
                take_turned_max(0, now + 1)
            if slot in (6, 10, 14) and has(n):
                take_heads({6: 0, 10: 1, 14: 2}[slot], now)
            if slot == 11 and has(n + 2):
                dve.wait_ge(A.v_full, now + 3)
                if begun(GROUPS * now):
                    dve.wait_ge(A.pv_done, GROUPS * now)
                dst = A.v_aug[:, new, :, :, 0:D]
                src = W.misc[:, :].rearrange("p (t h d) -> p t h d", t=TT, d=D)
                if layer == 0:
                    v.tensor_tensor(dst, src, W.bv[:, :].rearrange("p (h d) -> p h d", d=D).unsqueeze(1)
                                    .to_broadcast([P, TT, H, D]), ALU.add).then_inc(A.v_ready, 1)
                else:
                    v.tensor_copy(dst, src).then_inc(A.v_ready, 1)
            if slot == 15 and has(n + 1):
                split_max(1)

    route = RouteVector(dve, nc, R, A, W)
    v.memset(R.seen[:, :], 0.0).then_inc(R.seen_ready, 1)
    v.memset(A.k_stack[:, :, :, :, :], 0.0)
    v.memset(A.v_aug[:, :, :, :, :], 0.0).then_inc(A.v_zeroed, 1)
    dve.wait_ge(A.v_zeroed, layer + 1)
    v.memset(A.v_aug[:, :, :, :, D:D + 1], 1.0).then_inc(A.rows_set, 1)
    sweep(dve, body, -2 if layer == 0 else -3)


def attention_gpsimd(pool, nc, A, W, R, Q=None):
    g_ = nc.gpsimd
    layer = R.layer
    first = layer * B

    def body(n, turn):
        now = n + first
        cur, nxt = turn, (turn + 1) % NB

        def rstd(k, var_sem, rstd_sem, count, step_sem):
            pool.wait_ge(var_sem, count)
            pool.sem_inc(W.passed, 1)
            g_.tensor_scalar(A.rstd[:, k, :], A.mean_var[:, k, :, 1], EPS, None, ALU.add).then_inc(step_sem, 1)
            pool.wait_ge(step_sem, count)
            g_.tensor_tensor(A.rstd[:, k, :], A.rstd[:, k, :], W.minus_half[:, 0:TT], ALU.pow).then_inc(rstd_sem, 1)

        def rest(which, ready):
            pool.wait_ge(ready, now + 3)
            if begun(2 * (now + 2) + which):
                pool.wait_ge(A.parts_ready, 2 * (now + 2) + which)
            g_.tensor_tensor(A.rest[:, :], A.full[:, which, :], A.part[:, which, 0, :],
                             ALU.subtract).then_inc(A.rest_ready, 1)

        def last_part(which):
            pool.wait_ge(A.mid_ready, 2 * (now + 2) + which + 1)
            g_.tensor_tensor(A.part[:, which, 2, :], A.rest[:, :], A.part[:, which, 1, :],
                             ALU.subtract).then_inc(A.parts_ready, 1)

        for slot in range(SLOTS):
            if slot == 0 and has(n + 2):
                if begun(now + 2):
                    pool.wait_ge(A.xn_ready, now + 2)
                    pool.sem_inc(W.passed, 1)
                rstd(0, A.xn_var, A.xn_rstd, now + 3, A.xn_eps)
            if slot == 8 and has(n - 1):
                rstd(1, A.y_var, A.y_rstd, now, A.y_eps)
            if slot == 5 and has(n + 2):
                rest(0, A.q_ready)
            if slot == 7 and has(n + 2):
                last_part(0)
                rest(1, A.k_ready)
            if slot == 9 and has(n + 2):
                last_part(1)
            if slot == 0 and has(n - 2):
                route_gpsimd_rstd(pool, nc, R, W, R.norms * (n - 2) + 1)
            if slot == 1 and has(n - 2) and layer == 0:
                route_gpsimd_rstd(pool, nc, R, W, R.norms * (n - 2) + 2)
            if slot == 8 and has(n - 2) and layer == 0:
                route_gpsimd_rstd(pool, nc, R, W, R.norms * (n - 2) + 3)
            if slot in (2, 3, 4, 6, 10, 11) and has(n - 2) and layer == 0:
                route_gpsimd_scale(pool, nc, R, W, n - 2, nxt, (2, 3, 4, 6, 10, 11).index(slot))
            if slot >= 8 and has(n - 3):
                scatter(pool, nc, R, W, n - 3, cur, slot - 8)
            if 1 <= slot <= 8 and has(n + 3) and layer == 1:
                gather(pool, nc, Q, W, n + 3, turn, slot - 1)
            if slot == 12 and has(n + 3) and layer == 1:
                collect_rstd(pool, nc, Q, W, n + 3)

    sweep(pool, body, -2 if layer == 0 else -3)


def attention_sync(sp, nc, A, W, R, Q=None):
    layer = R.layer
    first = layer * B
    wide = PAIRS * T

    def body(n, turn):
        now = n + first
        cur, nxt, new = turn, (turn + 1) % NB, (turn + 2) % NB

        def maxima(ph, at, buf):
            sp.wait_ge(A.maxt_ready, 2 * at + ph + 1)
            sp.sem_inc(W.passed, 1)
            if begun(32 * (2 * at + ph)):
                sp.wait_ge(A.max_loaded, 32 * (2 * at + ph))
                sp.sem_inc(W.passed, 1)
            sp.dma_start(W.max_dram[ph], A.max_t[:, ph, :]).then_inc(A.max_written, 16)
            sp.wait_ge(A.max_written, 16 * (2 * at + ph + 1))
            sp.sem_inc(W.passed, 1)
            for half in range(2):
                sp.dma_start(
                    A.q_stack[64 * half + MAX_ROW:64 * half + MAX_ROW + 3, buf, 4 * ph:4 * ph + 4, :],
                    W.max_dram[ph].rearrange("(s h p) t -> h s p t", s=3, h=2)[half],
                ).then_inc(A.max_loaded, 16)

        if has(n + 3) and layer == 1:
            collect_load(sp, Q, W, n + 3)
        if has(n):
            maxima(1, now, cur)
        if has(n - 2):
            b, src = n - 2, R.total[:, :, :] if layer == 0 else R.rows[:, nxt, :, :]
            if layer == 1:
                sp.wait_ge(R.rows_ready, b + 1)
                sp.sem_inc(W.passed, 1)
                sp.dma_start(W.kept[b].rearrange("(t p) c -> p t c", p=P), src).then_inc(R.kept_written, 16)
        if has(n - 2) and layer == 0:
            sp.wait_ge(R.sum_ready, b + 1)
            sp.sem_inc(W.passed, 1)
            sp.dma_start(W.kept[b].rearrange("(t p) c -> p t c", p=P), src).then_inc(R.kept_written, 16)
        if has(n + 1):
            maxima(0, now + 1, nxt)
        if has(n + 2):
            if begun(LOADS * (now + 2)):
                sp.wait_ge(A.stack_loaded, LOADS * (now + 2))
                sp.sem_inc(W.passed, 1)
            for which in range(2):
                sp.wait_ge(A.parts_ready, 2 * (now + 2) + which + 1)
                sp.sem_inc(W.passed, 1)
                term = 0
                for k in range(3):
                    rows = W.stack_dram[which, term * D:(term + 3 - k) * D, :, :, :]
                    if which == 0:
                        src = A.part[:, 0, 0:3 - k, :]
                    else:
                        src = A.part[:, 1, k:k + 1, :].to_broadcast([P, 3 - k, T])
                    sp.dma_start(rows.rearrange("(s d) h p t -> (d h p) s t", d=D), src).then_inc(A.parts_written, 16)
                    term += 3 - k
            sp.wait_ge(A.parts_written, 2 * WRITES * (now + 3))
            sp.sem_inc(W.passed, 1)
            if begun(GROUPS * now):
                sp.wait_ge(A.scores_full, GROUPS * now)
                sp.sem_inc(W.passed, 1)
            for half in range(2):
                rows = slice(64 * half, 64 * half + 64)
                sp.dma_start(A.q_stack[rows, new, :, :], W.stack_dram[0, :, half]).then_inc(A.stack_loaded, 16)
                sp.dma_start(A.k_stack[rows, new, half, :, :], W.stack_dram[1, :, half]).then_inc(A.stack_loaded, 16)

    sp.dma_start(W.sorted_in[R.n * REGION:R.n * REGION + R.n * P, :].rearrange("(e p) c -> p e c", p=P),
                 spread(W.zeros[:, :], 1, [P, R.n, C])).then_inc(R.zeroed, 16)
    if begun(first):
        sp.wait_ge(A.x_ready, first)
        sp.sem_inc(W.passed, 1)
    sp.dma_start(W.stack_dram[0, ALIBI_ROW:64], W.q_rows).then_inc(A.rows_written, 16)
    sp.dma_start(W.stack_dram[1, ALIBI_ROW:64], W.k_rows[layer]).then_inc(A.rows_written, 16)
    sp.wait_ge(A.rows_written, 32 * (layer + 1))
    sp.wait_ge(A.rows_set, layer + 1)
    sp.sem_inc(W.passed, 1)
    sweep(sp, body, -2 if layer == 0 else -3)



TOP = 2
TILES = B * TT
REGION = B * T + P
MOVES = 16 * TT * TOP
MAX_E = 14


class Routing:

    def __init__(self, ctx, nc, bufs, layer, experts, width, table_steps, earlier_loads):
        self.layer, self.n, self.width = layer, experts, width
        self.table_start, self.table_steps = table_steps, table_steps + 12 + 2 * (experts - 1)
        self.chunks = width // P
        self.slots = TOP * TILES + experts
        self.weights_loads = 16 * (experts + 3) + earlier_loads
        self.norms = 3 if layer == 0 else 1
        def sb(name, shape):
            return ctx.enter_context(nc.sbuf_tensor(f"{name}{layer}", shape, F32))

        def sem(name):
            return ctx.enter_context(nc.semaphore(f"r{layer}_{name}"))

        (self.normed, self.second, self.total, self.got, self.kept, self.rows) = (bufs[name] for name in
            "normed second total got kept rows".split())
        (self.turned, self.stats, self.mean_var, self.rstd, self.neg_top, self.prob) = (bufs[name] for name in
            "turned stats mean_var rstd neg_top prob".split())
        (self.sum, self.best, self.best_at, self.best_f, self.hot, self.chosen) = (bufs[name] for name in
            "sum best best_at best_f hot chosen".split())
        (self.seen, self.new, self.rank, self.hot_rank, self.row_f, self.row) = (bufs[name] for name in
            "seen new rank hot_rank row_f row".split())
        (self.got_row, self.got_stats, self.got_mean_var, self.got_rstd, self.gap_i, self.gap) = (bufs[name] for name in
            "got_row got_stats got_mean_var got_rstd gap_i gap".split())
        (self.shift, self.tiles, self.tiles_i, self.marks, self.table_f, self.table) = (bufs[name] for name in
            "shift tiles tiles_i marks table_f table".split())
        (self.pad_row, self.passed, self.table_step, self.counts_full, self.tiles_ready,
         self.cum_full) = (bufs[name] for name in
            "pad_row passed table_step counts_full tiles_ready cum_full".split())
        (self.marks_ready, self.table_full, self.table_ready, self.pad_ready) = (bufs[name] for name in
            "marks_ready table_full table_ready pad_ready".split())
        self.row_all, self.weight = (sb(name, [P, TILES, TOP]) for name in ("row_all", "weight"))
        (self.place_step, self.var, self.rstd_ready, self.eps_added, self.step, self.rows_ready) = (sem(name) for name in
            "place_step var rstd_ready eps_added step rows_ready".split())
        (self.ft_full, self.ft_ready, self.logits_full, self.less_ready, self.exp_ready,
         self.chosen_ready) = (sem(name) for name in
            "ft_full ft_ready logits_full less_ready exp_ready chosen_ready".split())
        (self.ranks_full, self.ranks_taken, self.row_ready, self.seen_ready, self.scattered,
         self.kept_written) = (sem(name) for name in
            "ranks_full ranks_taken row_ready seen_ready scattered kept_written".split())
        (self.index_ready, self.got_step, self.got_var, self.got_eps, self.got_rstd_ready,
         self.x_collected) = (sem(name) for name in
            "index_ready got_step got_var got_eps got_rstd_ready x_collected".split())
        (self.padded, self.zeroed) = (sem(name) for name in
            "padded zeroed".split())
        if layer == 0:
            (self.second_ready, self.n_ready, self.n_step, self.total_step, self.total_ready,
             self.nt_full) = (sem(name) for name in
                "second_ready n_ready n_step total_step total_ready nt_full".split())
            (self.nt_ready, self.mix_full, self.sum_ready, self.rows_step) = (sem(name) for name in
                "nt_ready mix_full sum_ready rows_step".split())
        self.gathered = [ctx.enter_context(nc.semaphore(f"r{layer}_gathered{i}")) for i in range(layer + 1)]
        self.kept_loaded = [ctx.enter_context(nc.semaphore(f"r{layer}_kept_loaded{i}")) for i in range(layer + 1)]


def table_events(ctx, nc):
    names = "table_step counts_full tiles_ready cum_full marks_ready table_full table_ready pad_ready"
    return {name: ctx.enter_context(nc.semaphore("r_" + name)) for name in names.split()}


def routing_buffers(ctx, nc):
    def sb(name, shape, dt=F32):
        return ctx.enter_context(nc.sbuf_tensor("route_" + name, shape, dt))

    shared = sb("shared", [P, TT * (TOP + 1), C])
    return dict(
        normed=shared[:, 0:TT, :], second=shared[:, TT:2 * TT, :], total=shared[:, 2 * TT:3 * TT, :],
        got=[shared[:, 0:2 * TT, :].rearrange("p (t j) c -> p t j c", j=TOP)], kept=[shared[:, 2 * TT:3 * TT, :]],
        rows=sb("rows", [P, NB, TT, C]), turned=sb("turned", [P, T]),
        stats=sb("stats", [P, TT, 6]), mean_var=sb("mean_var", [P, TT, 2]), rstd=sb("rstd", [P, TT]),
        neg_top=sb("neg_top", [P, TT]), prob=sb("prob", [P, TT, MAX_E]), sum=sb("sum", [P, TT]),
        best=sb("best", [P, TT, 8]), best_at=sb("best_at", [P, TT, 8], U32), best_f=sb("best_f", [P, TT, TOP]),
        hot=sb("hot", [P, TT, TOP, MAX_E]), chosen=sb("chosen", [P, TT, MAX_E], BF16),
        seen=sb("seen", [P, MAX_E], BF16), new=sb("new", [P, MAX_E]), rank=sb("rank", [P, TT, MAX_E]),
        hot_rank=sb("hot_rank", [P, TT, TOP, MAX_E]), row_f=sb("row_f", [P, TT, TOP]),
        row=sb("row", [P, NB, TT, TOP], U32), got_row=sb("got_row", [P, NB, TT, TOP], U32),
        
        got_stats=sb("got_stats", [P, TT, 6]), got_mean_var=sb("got_mean_var", [P, TT, 2]),
        got_rstd=sb("got_rstd", [P, TT]),
        gap_i=sb("gap_i", [P, 2, MAX_E], I32), gap=sb("gap", [P, MAX_E]), shift=sb("shift", [P, TILES * TOP]),
        tiles=sb("tiles", [MAX_E, 4]), tiles_i=sb("tiles_i", [MAX_E, 2], I32),
        marks=sb("marks", [MAX_E, TOP * TILES + MAX_E]), table_f=sb("table_f", [1, 2, TOP * TILES + MAX_E]),
        table=sb("table", [1, 2, TOP * TILES + MAX_E], I32), pad_row=sb("pad_row", [P, MAX_E], U32),
    )


def spread(ap, axis, shape):
    return ap.unsqueeze(axis).to_broadcast(shape)


def tiles_mean_var(dve, nc, R, src, stats, mean_var, step_sem, count, var_sem):
    for t in range(TT):
        last = nc.vector.bn_stats(stats[:, t, :], src(t))
    last.then_inc(step_sem, 1)
    dve.wait_ge(step_sem, count)
    dve.sem_inc(R.passed, 1)
    for t in range(TT):
        last = nc.vector.bn_aggr(mean_var[:, t, :], stats[:, t, :])
    last.then_inc(var_sem, 1)


def tiles_normalise(nc, dst, src, mean_var, rstd):
    for t in range(TT):
        last = nc.vector.tensor_scalar(dst(t), src(t), mean_var[:, t, 0:1], rstd[:, t:t + 1],
                                       ALU.subtract, ALU.mult)
    return last


class RouteVector:

    STEPS = (12, 12)

    def __init__(self, dve, nc, R, A, W):
        self.dve, self.nc, self.R, self.A, self.W = dve, nc, R, A, W

    def stats(self, src, count):
        R = self.R
        tiles_mean_var(self.dve, self.nc, R, src, R.stats, R.mean_var, R.step, count, R.var)

    def x_stats(self, b):
        dve, R, A = self.dve, self.R, self.A
        dve.wait_ge(A.x_ready, b + 1 + R.layer * B)
        dve.sem_inc(R.passed, 1)
        self.stats(lambda t: A.x[:, b * TT + t, :], self.STEPS[R.layer] * b + 1)

    def x_norm(self, b, turn):
        dve, nc, R, A = self.dve, self.nc, self.R, self.A
        x = lambda t: A.x[:, b * TT + t, :]
        dve.wait_ge(R.rstd_ready, R.norms * b + 1)
        if R.layer == 1:
            if begun(16 * b):
                dve.wait_ge(R.kept_written, 16 * b)
            tiles_normalise(nc, lambda t: R.rows[:, turn, t, :], x, R.mean_var, R.rstd).then_inc(R.rows_ready, 1)
            return
        if begun(b):
            dve.wait_ge(R.total_ready, b)
        step = self.STEPS[0] * b + 1
        tiles_normalise(nc, lambda t: R.normed[:, t, :], x, R.mean_var, R.rstd).then_inc(R.step, 1)
        dve.wait_ge(R.step, step + 1)
        self.stats(lambda t: R.normed[:, t, :], step + 2)

    def second_norm(self, b):
        dve, nc, R = self.dve, self.nc, self.R
        dve.wait_ge(R.rstd_ready, 3 * b + 2)
        if begun(b):
            dve.wait_ge(R.rows_ready, b)
        tiles_normalise(nc, lambda t: R.second[:, t, :], lambda t: R.normed[:, t, :],
                        R.mean_var, R.rstd).then_inc(R.second_ready, 1)

    def mixed(self, b):
        dve, nc, R, W = self.dve, self.nc, self.R, self.W
        dve.wait_ge(R.mix_full, b + 1)
        dve.wait_ge(R.total_ready, b + 1)
        nc.vector.tensor_tensor(R.total[:, :, :], W.misc[:, :].rearrange("p (t c) -> p t c", t=TT),
                                R.total[:, :, :], ALU.add).then_inc(R.sum_ready, 1)
        dve.wait_ge(R.sum_ready, b + 1)
        dve.sem_inc(R.passed, 1)
        self.stats(lambda t: R.total[:, t, :], self.STEPS[0] * b + 4)

    def third_norm(self, b):
        dve, nc, R = self.dve, self.nc, self.R
        dve.wait_ge(R.rstd_ready, 3 * b + 3)
        dve.wait_ge(R.nt_full, b + 1)
        tiles_normalise(nc, lambda t: R.second[:, t, :], lambda t: R.total[:, t, :],
                        R.mean_var, R.rstd).then_inc(R.second_ready, 1)

    def logits(self, b):
        dve, nc, R, W = self.dve, self.nc, self.R, self.W
        E = R.n
        step = self.STEPS[R.layer] * b + (4 if R.layer == 0 else 1)
        logits = W.misc[:, 0:TT * E].rearrange("p (t e) -> p t e", t=TT)
        dve.wait_ge(R.logits_full, b + 1)
        nc.vector.tensor_reduce(R.neg_top[:, :], logits, AX.X, ALU.max, negate=True).then_inc(R.step, 1)
        dve.wait_ge(R.step, step + 1)
        nc.vector.tensor_tensor(R.prob[:, :, 0:E], logits, spread(R.neg_top[:, :], 2, [P, TT, E]),
                                ALU.add).then_inc(R.less_ready, 1)

    def choose(self, b):
        dve, nc, R = self.dve, self.nc, self.R
        v, E = nc.vector, R.n
        step = self.STEPS[R.layer] * b + (5 if R.layer == 0 else 2)
        prob = R.prob[:, :, 0:E]
        dve.wait_ge(R.exp_ready, b + 1)
        v.tensor_reduce(R.sum[:, :], prob, AX.X, ALU.add).then_inc(R.step, 1)
        dve.wait_ge(R.step, step + 1)
        v.reciprocal(R.sum[:, :], R.sum[:, :]).then_inc(R.step, 1)
        dve.wait_ge(R.step, step + 2)
        v.tensor_tensor(prob, prob, spread(R.sum[:, :], 2, [P, TT, E]), ALU.mult).then_inc(R.step, 1)
        dve.wait_ge(R.step, step + 3)
        dve.sem_inc(R.passed, 1)
        for t in range(TT):
            last = v.max(R.best[:, t, :], R.prob[:, t, 0:E])
        last.then_inc(R.step, 1)
        dve.wait_ge(R.step, step + 4)
        dve.sem_inc(R.passed, 1)
        for t in range(TT):
            last = v.max_index(R.best_at[:, t, :], R.best[:, t, :], R.prob[:, t, 0:E])
        last.then_inc(R.step, 1)
        dve.wait_ge(R.step, step + 5)
        v.tensor_copy(R.best_f[:, :, :], R.best_at[:, :, 0:TOP]).then_inc(R.step, 1)
        dve.wait_ge(R.step, step + 6)
        v.tensor_tensor(R.hot[:, :, :, 0:E],
                        self.W.numbers[:, 0:E].unsqueeze(1).unsqueeze(1).to_broadcast([P, TT, TOP, E]),
                        spread(R.best_f[:, :, :], 3, [P, TT, TOP, E]), ALU.is_equal).then_inc(R.step, 1)
        dve.wait_ge(R.step, step + 7)
        v.tensor_tensor(R.chosen[:, :, 0:E], R.hot[:, :, 0, 0:E], R.hot[:, :, 1, 0:E],
                        ALU.add).then_inc(R.chosen_ready, 1)
        best = R.best[:, :, 0:TOP]
        weight = R.weight[:, bass.ds(b * TT, TT), :]
        if R.layer == 0:
            v.tensor_copy(weight, best)
        else:
            v.tensor_tensor(R.sum[:, :], R.best[:, :, 0], R.best[:, :, 1], ALU.add).then_inc(R.step, 1)
            dve.wait_ge(R.step, step + 8)
            v.tensor_scalar(R.sum[:, :], R.sum[:, :], 1e-10, None, ALU.max).then_inc(R.step, 1)
            dve.wait_ge(R.step, step + 9)
            v.reciprocal(R.sum[:, :], R.sum[:, :]).then_inc(R.step, 1)
            dve.wait_ge(R.step, step + 10)
            v.tensor_tensor(weight, best, spread(R.sum[:, :], 2, [P, TT, TOP]), ALU.mult)

    def take_ranks(self, b):
        dve, nc, R, W = self.dve, self.nc, self.R, self.W
        v, E = nc.vector, R.n
        ranks = W.misc[:, 0:TT * E].rearrange("p (t e) -> p t e", t=TT)
        dve.wait_ge(R.ranks_full, b + 1)
        v.tensor_tensor(R.rank[:, :, 0:E], ranks, spread(W.regions[:, 0:E], 1, [P, TT, E]),
                        ALU.add).then_inc(R.ranks_taken, 1)

    def place(self, b, turn):
        dve, nc, R, W = self.dve, self.nc, self.R, self.W
        v, E = nc.vector, R.n
        step = 4 * b
        dve.wait_ge(R.ranks_taken, b + 1)
        v.tensor_tensor(R.hot_rank[:, :, :, 0:E], R.hot[:, :, :, 0:E],
                        spread(R.rank[:, :, 0:E], 2, [P, TT, TOP, E]), ALU.mult).then_inc(R.place_step, 1)
        dve.wait_ge(R.place_step, step + 1)
        v.tensor_reduce(R.row_f[:, :, :], R.hot_rank[:, :, :, 0:E], AX.X, ALU.add).then_inc(R.place_step, 1)
        dve.wait_ge(R.place_step, step + 2)
        if begun(MOVES * b):
            dve.wait_ge(R.scattered, MOVES * b)
        v.tensor_copy(R.row[:, turn, :, :], R.row_f[:, :, :]).then_inc(R.row_ready, 1)
        v.tensor_copy(R.row_all[:, bass.ds(b * TT, TT), :], R.row_f[:, :, :]).then_inc(R.place_step, 1)
        dve.wait_ge(R.place_step, step + 3)
        v.tensor_reduce(R.new[:, 0:E], R.chosen[:, :, 0:E].rearrange("p t e -> p e t"), AX.X, ALU.add).then_inc(R.place_step, 1)
        dve.wait_ge(R.place_step, step + 4)
        v.tensor_tensor(R.seen[:, 0:E], R.seen[:, 0:E], R.new[:, 0:E], ALU.add).then_inc(R.seen_ready, 1)


def route_gpsimd_rstd(pool, nc, R, W, count):
    pool.wait_ge(R.var, count)
    pool.sem_inc(W.passed, 1)
    nc.gpsimd.tensor_scalar(R.rstd[:, :], R.mean_var[:, :, 1], EPS, None, ALU.add).then_inc(R.eps_added, 1)
    pool.wait_ge(R.eps_added, count)
    nc.gpsimd.tensor_tensor(R.rstd[:, :], R.rstd[:, :], W.minus_half[:, 0:TT], ALU.pow).then_inc(R.rstd_ready, 1)


def route_gpsimd_scale(pool, nc, R, W, b, turn, step):
    def do(out, a, c, op, sem):
        nc.gpsimd.tensor_tensor(out, a, c, op).then_inc(sem, 1)

    row = lambda v: spread(v[:, :], 1, [P, TT, C])
    second, total = R.second[:, :, :], R.total[:, :, :]
    if step == 0:
        pool.wait_ge(R.second_ready, 2 * b + 1)
        do(second, second, row(W.g1), ALU.mult, R.n_step)
    elif step == 1:
        pool.wait_ge(R.n_step, b + 1)
        do(second, second, row(W.be1), ALU.add, R.n_ready)
    elif step == 2:
        pool.wait_ge(R.n_ready, b + 1)
        if begun(16 * b):
            pool.wait_ge(R.kept_written, 16 * b)
        do(total, R.normed[:, :, :], second, ALU.add, R.total_step)
    elif step == 3:
        pool.wait_ge(R.total_step, b + 1)
        do(total, total, row(W.mix_b), ALU.add, R.total_ready)
    elif step == 4:
        pool.wait_ge(R.second_ready, 2 * b + 2)
        do(second, second, row(W.g2), ALU.mult, R.rows_step)
    else:
        pool.wait_ge(R.rows_step, b + 1)
        do(R.rows[:, turn, :, :], second, row(W.be2), ALU.add, R.rows_ready)


def route_turn_n(pe, nc, R, W, b):
    pe.wait_ge(R.n_ready, b + 1)
    for t in range(TT):
        last = nc.tensor.transpose(W.misc[:, t * P:(t + 1) * P], R.second[:, t, :], W.ident[:, :])
    last.then_inc(R.nt_full, 1)
    return R.nt_ready, b + 1


def route_mix(pe, nc, R, W, b):
    pe.wait_ge(R.nt_ready, b + 1)
    for t in range(TT):
        rows = slice(t * P, (t + 1) * P)
        last = nc.tensor.matmul(W.misc[:, rows], R.turned[:, rows], W.mix[:, :], start=True, stop=True)
    last.then_inc(R.mix_full, 1)
    return R.sum_ready, b + 1


def route_turn_rows(pe, nc, R, W, b, turn):
    pe.wait_ge(R.rows_ready, b + 1)
    for t in range(TT):
        last = nc.tensor.transpose(W.misc[:, t * P:(t + 1) * P], R.rows[:, turn, t, :], W.ident[:, :])
    last.then_inc(R.ft_full, 1)
    return R.ft_ready, b + 1


def route_logits(pe, nc, R, W, b):
    E = R.n
    pe.wait_ge(R.ft_ready, b + 1)
    for t in range(TT):
        last = nc.tensor.matmul(W.misc[:, t * E:(t + 1) * E], R.turned[:, t * P:(t + 1) * P],
                                W.router[R.layer][:, :], start=True, stop=True)
    last.then_inc(R.logits_full, 1)
    return R.less_ready, b + 1


def route_ranks(pe, nc, R, W, b):
    mm, E = nc.tensor.matmul, R.n
    pe.wait_ge(R.chosen_ready, b + 1)
    pe.wait_ge(R.seen_ready, b + 1)
    ranks = W.misc[:, 0:TT * E].rearrange("p (t e) -> p t e", t=TT)
    mm(ranks, W.before[:, :], R.chosen[:, :, 0:E], start=True, stop=False, skip_group_check=True)
    for t in range(TT - 1):
        mm(ranks[:, t + 1:TT, :], W.ones16[:, :], spread(R.chosen[:, t, 0:E], 1, [P, TT - 1 - t, E]),
           start=False, stop=False, skip_group_check=True)
    mm(ranks, W.ones16[:, :], spread(R.seen[:, 0:E], 1, [P, TT, E]), start=False, stop=True,
       skip_group_check=True).then_inc(R.ranks_full, 1)
    return R.ranks_taken, b + 1


def route_scalar_n(act, nc, R, W, b):
    act.wait_ge(R.nt_full, b + 1)
    if begun(b):
        act.wait_ge(R.logits_full, b)
    nc.scalar.activation(R.turned[:, :], W.misc[:, :], ACT.Copy).then_inc(R.nt_ready, 1)


def route_scalar_rows(act, nc, R, W, b):
    act.wait_ge(R.ft_full, b + 1)
    if begun(b):
        act.wait_ge(R.logits_full, b)
    if R.layer == 0:
        act.wait_ge(R.mix_full, b + 1)
    nc.scalar.activation(R.turned[:, :], W.misc[:, :], ACT.Copy).then_inc(R.ft_ready, 1)


def route_scalar_exp(act, nc, R, W, b):
    act.wait_ge(R.less_ready, b + 1)
    prob = R.prob[:, :, 0:R.n]
    nc.scalar.activation(prob, prob, ACT.Exp).then_inc(R.exp_ready, 1)


def scatter(pool, nc, R, W, b, turn, k):
    t, j = divmod(k, TOP)
    if k == 0:
        pool.wait_ge(R.row_ready, b + 1)
        pool.sem_inc(W.passed, 1)
        pool.wait_ge(R.rows_ready, b + 1)
        pool.sem_inc(W.passed, 1)
    pool.indirect_dma_start(W.sorted_in, bass.IndirectOffsetOnAxis(ap=R.row[:, turn, t, j:j + 1], axis=0),
                            R.rows[:, turn, t, :], None).then_inc(R.scattered, 16)


def gather(pool, nc, R, W, b, turn, k, buf=0, bufs=1):
    t, j = divmod(k, TOP)
    if k == 0:
        pool.wait_ge(R.index_ready, b + 1)
        pool.sem_inc(W.passed, 1)
        if begun(b + 1 - bufs):
            pool.wait_ge(R.x_collected, b + 1 - bufs)
            pool.sem_inc(W.passed, 1)
    pool.indirect_dma_start(R.got[buf][:, t, j, :], None, W.sorted_out[0:R.slots * P, :],
                            bass.IndirectOffsetOnAxis(ap=R.got_row[:, turn, t, j:j + 1], axis=0)
                            ).then_inc(R.gathered[buf], 16)


def collect_index(dve, nc, R, b, turn):
    nc.vector.tensor_copy(R.got_row[:, turn, :, :], R.row_all[:, bass.ds(b * TT, TT), :]).then_inc(R.index_ready, 1)


COLLECT_STEPS = 4


def collect_sum(dve, nc, R, W, b, buf=0, use=None):
    v = nc.vector
    got, kept = R.got[buf], R.kept[buf]
    step = (COLLECT_STEPS + R.layer) * b
    use = b if use is None else use
    dve.wait_ge(R.gathered[buf], MOVES * (use + 1))
    dve.wait_ge(R.kept_loaded[buf], 16 * (use + 1))
    for j in range(TOP):
        for t in range(TT):
            last = v.scalar_tensor_tensor(kept[:, t, :], got[:, t, j, :], R.weight[:, b * TT + t, j:j + 1],
                                          kept[:, t, :], ALU.mult, ALU.add)
        last.then_inc(R.got_step, 1)
        dve.wait_ge(R.got_step, step + 1 + j)
    if R.layer == 1:
        v.tensor_scalar(kept[:, :, :], kept[:, :, :], 100.0, -100.0, ALU.min, ALU.max).then_inc(R.got_step, 1)
        dve.wait_ge(R.got_step, step + TOP + 1)
    tiles_mean_var(dve, nc, R, lambda t: kept[:, t, :], R.got_stats, R.got_mean_var, R.got_step,
                   step + TOP + 1 + R.layer, R.got_var)


def collect_add(dve, nc, R, A, b, buf=0):
    step = (COLLECT_STEPS + R.layer) * b + 3 + R.layer
    kept = lambda t: R.kept[buf][:, t, :]
    dve.wait_ge(R.got_rstd_ready, b + 1)
    tiles_normalise(nc, kept, kept, R.got_mean_var, R.got_rstd).then_inc(R.got_step, 1)
    dve.wait_ge(R.got_step, step + 1)
    rows = A.x[:, bass.ds(b * TT, TT), :]
    nc.vector.tensor_tensor(rows, rows, R.kept[buf][:, :, :], ALU.add).then_inc(R.x_collected, 1)


def collect_rstd(pool, nc, R, W, b):
    pool.wait_ge(R.got_var, b + 1)
    pool.sem_inc(W.passed, 1)
    nc.gpsimd.tensor_scalar(R.got_rstd[:, :], R.got_mean_var[:, :, 1], EPS, None, ALU.add).then_inc(R.got_eps, 1)
    pool.wait_ge(R.got_eps, b + 1)
    nc.gpsimd.tensor_tensor(R.got_rstd[:, :], R.got_rstd[:, :], W.minus_half[:, 0:TT],
                            ALU.pow).then_inc(R.got_rstd_ready, 1)


def collect_load(sp, R, W, b, buf=0, bufs=1):
    if begun(b + 1 - bufs):
        sp.wait_ge(R.x_collected, b + 1 - bufs)
        sp.sem_inc(W.passed, 1)
    sp.dma_start(R.kept[buf][:, :, :], W.kept[b].rearrange("(t p) c -> p t c", p=P)).then_inc(R.kept_loaded[buf], 16)




class Experts:

    def __init__(self, stack, nc, R, events, before):
        F, n = R.width, R.n

        def sb(name, shape, dt=F32):
            return stack.enter_context(nc.sbuf_tensor(f"x{R.layer}_{name}", shape, dt))

        self.w1 = sb("w1", [P, n, F])
        self.tail = sb("tail", [P, n, R.chunks * C + R.chunks + C])
        self.tile_w1 = sb("tile_w1", [P, 2, F])
        self.tile_tail = sb("tile_tail", [P, 4, R.chunks * C + R.chunks + C])
        self.rows = sb("rows", [P, 4, C])
        self.rows_t = sb("rows_t", [P, 2, P])
        self.hidden = sb("hidden", [P, 2, F])
        self.out = sb("out", [P, 2, C])
        (self.weights_loaded, self.turned_full, self.turned_ready, self.up_full, self.w1_ready,
         self.tail_ready) = (events[name] for name in
            "weights_loaded turned_full turned_ready up_full w1_ready tail_ready".split())
        (self.hidden_ready, self.down_full, self.out_ready, self.rows_loaded,
         self.out_written) = (events[name] for name in
            "hidden_ready down_full out_ready rows_loaded out_written".split())
        self.before = before


def tile_events(ctx, nc):
    def sem(name):
        return ctx.enter_context(nc.semaphore("x_" + name))

    names = "weights_loaded turned_full turned_ready up_full w1_ready tail_ready hidden_ready down_full out_ready"
    events = {name: sem(name) for name in names.split()}
    events["rows_loaded"] = [sem(f"rows_loaded{i}") for i in range(4)]
    events["out_written"] = [sem(f"out_written{i}") for i in range(2)]
    return events


def tile_sweep(eng, R, body, ahead):
    lo, hi = 4, R.slots - ahead
    hi -= (hi - lo) % 4
    for s in range(-ahead, lo):
        body(s, s, 0)
    with eng.Fori(0, (hi - lo) // 4) as i:
        for k in range(lo, lo + 4):
            body(i * 4 + k, k, i)
    for s in range(hi, R.slots):
        body(s, s, 0)


def is_slot(R, s):
    return not isinstance(s, int) or 0 <= s < R.slots


def expert_of(eng, R, s):
    return eng.value_load(R.table[0:1, 0, bass.ds(s, 1)], min_val=0, max_val=R.n - 1)


def experts_tensor(pe, nc, R, X, W):
    mm, tr = nc.tensor.matmul, nc.tensor.transpose
    turned = [W.o_ps, W.misc]

    def body(s, k, i4):
        c = s + X.before
        if is_slot(R, s + 2):
            i = (k + 2) % 2
            pe.wait_ge(X.rows_loaded[(k + 2) % 4], 4 * X.before + 16 * (i4 + (k + 2) // 4 + 1))
            if begun(c + 1):
                pe.wait_ge(X.turned_ready, c + 1)
            tr(turned[i][:, 0:P], X.rows[:, (k + 2) % 4, :], W.ident[:, :]).then_inc(X.turned_full, 1)
        if is_slot(R, s + 1):
            i = (k + 1) % 2
            pe.wait_ge(X.w1_ready, c + 2)
            pe.wait_ge(X.turned_ready, c + 2)
            if begun(c):
                pe.wait_ge(X.hidden_ready, c)
            for f in range(R.chunks):
                last = mm(W.s_ps[:, i, f * P:(f + 1) * P], X.tile_w1[:, i, f * P:(f + 1) * P],
                          X.rows_t[:, i, :], start=True, stop=True)
            last.then_inc(X.up_full, 1)
        if is_slot(R, s):
            i = k % 2
            pe.wait_ge(X.hidden_ready, c + 1)
            if begun(c - 1):
                pe.wait_ge(X.out_ready, c - 1)
            for f in range(R.chunks):
                last = mm(W.m_ps[:, i, 0:C], X.hidden[:, i, f * P:(f + 1) * P],
                          X.tile_tail[:, k % 4, f * C:(f + 1) * C],
                          start=(f == 0), stop=(f == R.chunks - 1))
            last.then_inc(X.down_full, 1)

    tile_sweep(pe, R, body, 2)


def experts_scalar(act, nc, R, X, W):
    func = ACT.Silu if R.layer == 0 else ACT.Gelu

    def body(s, k, i4):
        c = s + X.before
        if is_slot(R, s + 1):
            i = (k + 1) % 2
            act.wait_ge(X.tail_ready, c + 2)
            act.wait_ge(X.up_full, c + 2)
            if begun(c):
                act.wait_ge(X.down_full, c)
            for f in range(R.chunks):
                last = nc.scalar.activation(X.hidden[:, i, f * P:(f + 1) * P], W.s_ps[:, i, f * P:(f + 1) * P], func,
                                            bias=X.tile_tail[:, (k + 1) % 4, R.chunks * C + f:R.chunks * C + f + 1])
            last.then_inc(X.hidden_ready, 1)

    tile_sweep(act, R, body, 1)


def experts_vector(dve, nc, R, X, W):
    v = nc.vector
    turned = [W.o_ps, W.misc]
    dve.wait_ge(X.weights_loaded, R.weights_loads)

    def body(s, k, i4):
        c = s + X.before
        if is_slot(R, s + 2):
            i = (k + 2) % 2
            e = expert_of(dve, R, s + 2)
            if begun(c - 1):
                dve.wait_ge(X.out_ready, c - 1)
            v.tensor_copy(X.tile_tail[:, (k + 2) % 4, :], X.tail[:, bass.ds(e, 1), :]
                          .rearrange("p a f -> p (a f)")).then_inc(X.tail_ready, 1)
            dve.wait_ge(X.turned_full, c + 3)
            if begun(c + 1):
                dve.wait_ge(X.up_full, c + 1)
            v.tensor_copy(X.rows_t[:, i, :], turned[i][:, 0:P]).then_inc(X.turned_ready, 1)
        if is_slot(R, s):
            i = k % 2
            dve.wait_ge(X.down_full, c + 1)
            written = 8 * X.before + 16 * (i4 * 2 + k // 2)
            if begun(written):
                dve.wait_ge(X.out_written[i], written)
            v.tensor_tensor(X.out[:, i, :], W.m_ps[:, i, 0:C], X.tile_tail[:, k % 4, R.chunks * (C + 1):],
                            ALU.add).then_inc(X.out_ready, 1)

    tile_sweep(dve, R, body, 2)


def experts_gpsimd(pool, nc, R, X, W):
    pool.wait_ge(X.weights_loaded, R.weights_loads)

    def body(s, k, i4):
        c = s + X.before
        if is_slot(R, s + 2):
            e = expert_of(pool, R, s + 2)
            if begun(c + 1):
                pool.wait_ge(X.up_full, c + 1)
                pool.sem_inc(W.passed, 1)
            nc.gpsimd.tensor_copy(X.tile_w1[:, (k + 2) % 2, :], X.w1[:, bass.ds(e, 1), :]
                                  .rearrange("p a f -> p (a f)")).then_inc(X.w1_ready, 1)

    tile_sweep(pool, R, body, 2)


AHEAD = 5


def experts_sync(sp, nc, R, X, W):
    def body(s, k, i4):
        c = s + X.before
        if is_slot(R, s + AHEAD):
            row = sp.value_load(R.table[0:1, 1, bass.ds(s + AHEAD, 1)], min_val=0,
                                max_val=R.n * REGION + (R.n - 1) * P)
            turned = c + AHEAD - 3
            if s >= -1 if isinstance(s, int) else True:
                sp.wait_ge(X.turned_full, turned)
                sp.sem_inc(W.passed, 1)
            sp.dma_start(X.rows[:, (k + AHEAD) % 4, :], W.sorted_in[bass.ds(row, P), :]
                         ).then_inc(X.rows_loaded[(k + AHEAD) % 4], 16)
        if is_slot(R, s):
            sp.wait_ge(X.out_ready, c + 1)
            sp.sem_inc(W.passed, 1)
            sp.dma_start(W.sorted_out[bass.ds(s * P, P), :], X.out[:, k % 2, :]
                         ).then_inc(X.out_written[k % 2], 16)

    tile_sweep(sp, R, body, AHEAD)




def table_tensor(pe, nc, R, W):
    mm = nc.tensor.matmul
    E, S = R.n, R.slots
    pe.wait_ge(R.seen_ready, B + 1)
    mm(W.misc[0:E, 0:1], R.seen[:, 0:E], W.ones16[:, 0:1], start=True, stop=True)
    mm(W.misc[:, 8:8 + E], W.ones16[:, :], R.seen[:, 0:E], start=True, stop=True).then_inc(R.counts_full, 1)
    pe.wait_ge(R.tiles_ready, R.layer + 1)
    mm(W.misc[0:E, 64:65], W.upto[0:E, 0:E], R.tiles[0:E, 1:2], start=True, stop=True).then_inc(R.cum_full, 1)
    pe.wait_ge(R.marks_ready, R.layer + 1)
    mm(W.misc[0:1, 128:128 + S], W.ones32[0:E, 0:1], R.marks[0:E, 0:S], start=True, stop=True)
    mm(W.misc[0:1, 320:320 + S], R.tiles[0:E, 1:2], R.marks[0:E, 0:S], start=True, stop=True).then_inc(R.table_full, 1)


def table_vector(dve, nc, R, W):
    v = nc.vector
    E, S = R.n, R.slots
    step = R.table_start
    dve.wait_ge(R.counts_full, R.layer + 1)
    v.tensor_tensor(R.rank[:, 0, 0:E], W.misc[:, 8:8 + E], W.regions[:, 0:E], ALU.add).then_inc(R.table_step, 1)
    dve.wait_ge(R.table_step, step + 1)
    v.tensor_scalar(R.pad_row[:, 0:E], R.rank[:, 0, 0:E], W.partition[:, 0:1], None, ALU.add).then_inc(R.pad_ready, 1)
    v.tensor_scalar(R.gap_i[:, 0, 0:E], W.misc[:, 8:8 + E], float(P - 1), None, ALU.add).then_inc(R.table_step, 1)
    dve.wait_ge(R.table_step, step + 2)
    v.tensor_scalar(R.tiles_i[0:E, 0:1], W.misc[0:E, 0:1], float(P - 1), None, ALU.add).then_inc(R.table_step, 1)
    dve.wait_ge(R.table_step, step + 3)
    v.tensor_scalar(R.tiles_i[0:E, 1:2], R.tiles_i[0:E, 0:1], 7, None, ALU.logical_shift_right).then_inc(R.table_step, 1)
    dve.wait_ge(R.table_step, step + 4)
    v.tensor_copy(R.tiles[0:E, 1:2], R.tiles_i[0:E, 1:2]).then_inc(R.tiles_ready, 1)
    dve.wait_ge(R.cum_full, R.layer + 1)
    v.tensor_copy(R.tiles[0:E, 2:3], W.misc[0:E, 64:65]).then_inc(R.table_step, 1)
    dve.wait_ge(R.table_step, step + 5)
    v.tensor_scalar(R.marks[0:E, 0:S], W.numbers[0:E, 0:S], R.tiles[0:E, 2:3], None, ALU.is_ge).then_inc(R.marks_ready, 1)
    dve.wait_ge(R.table_full, R.layer + 1)
    expert, before = R.table_f[0:1, 0, 0:S], R.table_f[0:1, 1, 0:S]
    v.tensor_copy(expert, W.misc[0:1, 128:128 + S]).then_inc(R.table_step, 1)
    dve.wait_ge(R.table_step, step + 6)
    v.tensor_tensor(before, W.numbers[0:1, 0:S], W.misc[0:1, 320:320 + S], ALU.subtract).then_inc(R.table_step, 1)
    dve.wait_ge(R.table_step, step + 7)
    v.tensor_scalar(before, before, float(P), None, ALU.mult).then_inc(R.table_step, 1)
    dve.wait_ge(R.table_step, step + 8)
    v.scalar_tensor_tensor(before, expert, float(REGION), before, ALU.mult, ALU.add).then_inc(R.table_step, 1)
    dve.wait_ge(R.table_step, step + 9)
    v.tensor_scalar(R.table[0:1, 0, 0:S], expert, float(E - 1), None, ALU.min)
    v.tensor_copy(R.table[0:1, 1, 0:S], before).then_inc(R.table_ready, 1)


def result_rows(dve, nc, R, W):
    v, E = nc.vector, R.n
    step = R.table_start + 9
    gap, rows = R.gap[:, 0:E], R.row_all[:, :, :].rearrange("p t j -> p (t j)")
    v.tensor_scalar(R.gap_i[:, 1, 0:E], R.gap_i[:, 0, 0:E], 7, None, ALU.logical_shift_right).then_inc(R.table_step, 1)
    dve.wait_ge(R.table_step, step + 1)
    v.tensor_copy(gap, R.gap_i[:, 1, 0:E]).then_inc(R.table_step, 1)
    dve.wait_ge(R.table_step, step + 2)
    v.tensor_scalar(gap, gap, -float(P), float(REGION), ALU.mult, ALU.add).then_inc(R.table_step, 1)
    dve.wait_ge(R.table_step, step + 3)
    for e in range(E - 1, 0, -1):
        v.scalar_tensor_tensor(R.shift[:, :], rows, float(e * REGION),
                               R.gap[:, e - 1:e].to_broadcast([P, TILES * TOP]), ALU.is_ge, ALU.mult).then_inc(R.table_step, 1)
        dve.wait_ge(R.table_step, step + 3 + 2 * (E - e) - 1)
        v.tensor_tensor(rows, rows, R.shift[:, :], ALU.subtract).then_inc(R.table_step, 1)
        dve.wait_ge(R.table_step, step + 3 + 2 * (E - e))


def table_gpsimd(pool, nc, R, W):
    pool.wait_ge(R.pad_ready, R.layer + 1)
    for e in range(R.n):
        pool.indirect_dma_start(W.sorted_in, bass.IndirectOffsetOnAxis(ap=R.pad_row[:, e:e + 1], axis=0),
                                W.zeros[:, :], None).then_inc(R.padded, 16)


def table_wait(eng, R, loads=False):
    eng.wait_ge(R.table_ready, R.layer + 1)
    if loads:
        eng.wait_ge(R.scattered, MOVES * B)
        eng.wait_ge(R.padded, 16 * R.n)
        eng.wait_ge(R.zeroed, 16)


def experts_done(eng, R, X):
    for i in range(2):
        eng.wait_ge(X.out_written[i], 8 * (X.before + R.slots))


def load_weights(sp, nc, R, X, W):
    w1, b1, w2_dram, b2 = W.experts[R.layer]
    w2, bias1, bias2 = X.tail[:, :, 0:R.chunks * C], X.tail[:, :, R.chunks * C:R.chunks * (C + 1)], X.tail[:, :, R.chunks * (C + 1):]
    sp.dma_start(X.w1[:, :, :], w1.rearrange("e p f -> p e f")).then_inc(X.weights_loaded, 16)
    for e in range(R.n):
        sp.dma_start(w2[:, e, :].rearrange("p (k c) -> p k c", c=C),
                     w2_dram[e].rearrange("(k p) c -> p k c", p=P)).then_inc(X.weights_loaded, 16)
    sp.dma_start(bias1, b1).then_inc(X.weights_loaded, 16)
    sp.dma_start(bias2, b2.partition_broadcast(P)).then_inc(X.weights_loaded, 16)


def final_sweep(eng, body):
    for b in (-1, 0, 1):
        body(b, b, 0)
    with eng.Fori(0, (B - 4) // 2) as i:
        for u in (2, 3):
            body(i * 2 + u, u, i)
    for b in range(B - 2, B + 1):
        body(b, b, 0)


def sandwich(nc, x, consts, weights, out):
    with ExitStack() as ctx:
        def sem(name):
            return ctx.enter_context(nc.semaphore(name))

        class W:
            pass

        loads = []

        def sb(stack, name, shape, dt=F32):
            return stack.enter_context(nc.sbuf_tensor(name + "_sb", shape, dt))

        def constant(name, ap, rows=None):
            if rows is not None:
                ap = ap.partition_broadcast(rows)
            tile = sb(ctx, name, list(ap.shape), ap.dtype)
            loads.append((tile, ap))
            return tile

        x_sb = sb(ctx, "x", [P, TILES, C])
        (W.ident, W.ident16, W.causal, W.before, W.ones16, W.ones32) = (constant(name, consts[name]) for name in
            "ident ident16 causal before ones16 ones32".split())
        (W.zeros, W.upto, W.partition, W.numbers, W.regions, W.minus_half) = (constant(name, consts[name]) for name in
            "zeros upto partition numbers regions minus_half".split())
        W.wq = [constant(f"wq{i}", weights[f"wq{i}"]) for i in range(2)]
        W.wo = [constant(f"wo{i}", weights[f"wo{i}"]) for i in range(2)]
        W.router = [constant(f"router{i}", weights[f"router{i}"]) for i in range(2)]
        (W.wkd, W.wku, W.wk1, W.wv1, W.bq, W.bk) = (constant(name, weights[name]) for name in
            "wkd wku wk1 wv1 bq bk".split())
        (W.bkd, W.mix) = (constant(name, weights[name]) for name in
            "bkd mix".split())
        (W.bv, W.bo, W.g1, W.be1, W.mix_b, W.g2) = (constant(name, weights[name], P) for name in
            "bv bo g1 be1 mix_b g2".split())
        W.be2 = constant("be2", weights["be2"], P)
        W.q_rows, W.k_rows = consts["q_rows"], consts["k_rows"]
        W.experts = weights["experts"]

        def dram(name, shape, dt=F32):
            return nc.dram_tensor(name, shape, dt, kind="Internal").ap()

        W.stack_dram = dram("stack_dram", [2, 64, 2, PAIRS, T], BF16)
        W.max_dram = dram("max_dram", [2, 24, T], BF16)
        W.kept = dram("kept_dram", [B, T, C])
        W.sorted_in = dram("sorted_in", [MAX_E * (REGION + P), C])
        W.sorted_out = dram("sorted_out", [(TOP * TILES + MAX_E) * P, C])

        W.s_ps = ctx.enter_context(nc.psum_tensor("s_ps", [P, 4, T], F32))
        W.m_ps = ctx.enter_context(nc.psum_tensor("m_ps", [P, 2, T], F32))
        W.o_ps = ctx.enter_context(nc.psum_tensor("o_ps", [P, T], F32))
        W.misc = ctx.enter_context(nc.psum_tensor("misc", [P, T], F32))

        constants_loaded, x_first, x_rest, stored = (sem(s) for s in ("constants_loaded", "x_first", "x_rest", "stored"))
        W.passed = sem("passed")
        all_loaded = (constants_loaded, 16 * len(loads))
        bufs = routing_buffers(ctx, nc)
        bufs["passed"] = W.passed
        bufs.update(table_events(ctx, nc))
        tiles = tile_events(ctx, nc)
        R = []
        for layer in range(2):
            experts, _, width = weights["experts"][layer][0].shape
            R.append(Routing(ctx, nc, bufs, layer, experts, width, R[0].table_steps if layer == 1 else 0,
                             R[0].weights_loads if layer == 1 else 0))
        with ExitStack() as stack:
            A = Attention(stack, ctx, nc, x_sb)
        X = []
        for layer in range(2):
            with ExitStack() as stack:
                X.append(Experts(stack, nc, R[layer], tiles, R[0].slots if layer == 1 else 0))
                if layer == 1:
                    last_got = [sb(stack, f"last_got{i}", [P, TT, TOP, C]) for i in range(2)]
                    last_kept = [sb(stack, f"last_kept{i}", [P, TT, C]) for i in range(2)]

        def wait_for_x(eng, layer, b):
            if layer == 1:
                eng.wait_ge(R[0].x_collected, b + 1)
                eng.sem_inc(W.passed, 1)
            elif isinstance(b, int) and b < 2:
                eng.wait_ge(x_first, 16 * 2)
            else:
                eng.wait_ge(x_rest, 16)

        W.wait_for_x = wait_for_x
        x_view = x.rearrange("b (t p) c -> p (b t) c", p=P)
        out_view = out.rearrange("b (t p) c -> p (b t) c", p=P)
        block = ctx.enter_context(nc.Block())

        @block.sync
        def _(sp):
            for b in range(2):
                sp.dma_start(x_sb[:, b * TT:(b + 1) * TT, :], x_view[:, b * TT:(b + 1) * TT, :]).then_inc(x_first, 16)
            for tile, ap in loads:
                sp.dma_start(tile[:], ap).then_inc(constants_loaded, 16)
            sp.dma_start(x_sb[:, 2 * TT:, :], x_view[:, 2 * TT:, :]).then_inc(x_rest, 16)
            sp.wait_ge(*all_loaded)
            for layer in range(2):
                attention_sync(sp, nc, A, W, R[layer], R[0])
                sp.wait_ge(R[layer].table_ready, layer + 1)
                load_weights(sp, nc, R[layer], X[layer], W)
                table_wait(sp, R[layer], True)
                experts_sync(sp, nc, R[layer], X[layer], W)
                experts_done(sp, R[layer], X[layer])

            def body(b, k, i):
                if has(b + 1):
                    collect_load(sp, R[1], W, b + 1, (k + 1) % 2, 2)
                if has(b - 1):
                    sp.wait_ge(R[1].x_collected, b)
                    sp.sem_inc(W.passed, 1)
                    sp.dma_start(out_view[:, bass.ds((b - 1) * TT, TT), :],
                                 x_sb[:, bass.ds((b - 1) * TT, TT), :]).then_inc(stored, 16)

            R[1].kept = last_kept
            final_sweep(sp, body)
            sp.wait_ge(stored, 16 * B)

        @block.tensor
        def _(pe):
            pe.wait_ge(*all_loaded)
            for layer in range(2):
                attention_tensor(pe, nc, A, W, R[layer])
                table_tensor(pe, nc, R[layer], W)
                table_wait(pe, R[layer])
                experts_tensor(pe, nc, R[layer], X[layer], W)

        @block.scalar
        def _(act):
            act.wait_ge(*all_loaded)
            for layer in range(2):
                attention_scalar(act, nc, A, W, R[layer])
                experts_scalar(act, nc, R[layer], X[layer], W)

        @block.vector
        def _(dve):
            dve.wait_ge(*all_loaded)
            R[1].kept = bufs["kept"]
            for layer in range(2):
                if layer == 1:
                    experts_done(dve, R[0], X[0])
                attention_vector(dve, nc, A, W, R[layer], R[0])
                table_vector(dve, nc, R[layer], W)
                table_wait(dve, R[layer])
                result_rows(dve, nc, R[layer], W)
                experts_vector(dve, nc, R[layer], X[layer], W)
            experts_done(dve, R[1], X[1])
            R[1].got, R[1].kept = last_got, last_kept

            def body(b, k, i):
                if has(b + 1):
                    collect_index(dve, nc, R[1], b + 1, (k + 1) % 2)
                if has(b):
                    collect_sum(dve, nc, R[1], W, b, k % 2, i + k // 2)
                    collect_add(dve, nc, R[1], A, b, k % 2)

            final_sweep(dve, body)

        @block.gpsimd
        def _(pool):
            pool.wait_ge(*all_loaded)
            for layer in range(2):
                if layer == 1:
                    experts_done(pool, R[0], X[0])
                attention_gpsimd(pool, nc, A, W, R[layer], R[0])
                table_gpsimd(pool, nc, R[layer], W)
                table_wait(pool, R[layer])
                experts_gpsimd(pool, nc, R[layer], X[layer], W)
            experts_done(pool, R[1], X[1])
            R[1].got = last_got

            def body(b, k, i):
                if has(b + 1):
                    for copy in range(TT * TOP):
                        gather(pool, nc, R[1], W, b + 1, (k + 1) % 2, copy, (k + 1) % 2, 2)
                if has(b):
                    collect_rstd(pool, nc, R[1], W, b)

            final_sweep(pool, body)




def heads_apart(a, np):
    a = np.asarray(a)
    lead = a.shape[:-1]
    a = a.reshape(*lead, PAIRS, 2, D)
    return np.ascontiguousarray(np.swapaxes(a, -1, -3).reshape(*lead, C))


def by_partition(b, np):
    b = np.asarray(b)
    return np.ascontiguousarray(b.reshape(b.shape[0], -1, P).transpose(2, 0, 1))


def shape_constants(np, bf16):
    at = np.arange(P)
    q_rows = np.zeros((16, 2, PAIRS, T))
    q_rows[0:3] = 1
    k_rows = np.zeros((2, 16, 2, PAIRS, T))
    k_rows[:, 3:6] = 1
    base = np.float32(2.0 ** (-8.0 / H))
    slopes = np.array([base ** i for i in range(1, H + 1)], np.float32).astype(np.float64)
    for half in range(2):
        bias = slopes[half::2][:, None] * np.arange(T)[None, :] / SCALE
        for part in range(3):
            k_rows[1, part, half] = bias.astype(bf16).astype(np.float64)
            bias = bias - k_rows[1, part, half]
    f = np.float32
    slots = TOP * TILES + MAX_E
    return dict(
        ident=np.eye(P, dtype=f), ident16=np.eye(P).astype(bf16),
        causal=np.where(at[None, :] > at[:, None], NEG, 0.0).astype(bf16),
        before=(at[:, None] < at[None, :]).astype(bf16), ones16=np.ones((P, P)).astype(bf16),
        ones32=np.ones((P, 2), f), zeros=np.zeros((P, C), f),
        upto=(np.arange(MAX_E)[:, None] <= np.arange(MAX_E)[None, :]).astype(f),
        partition=at[:, None].astype(f), numbers=np.tile(np.arange(slots, dtype=f), (P, 1)),
        regions=np.tile(np.arange(MAX_E, dtype=f) * REGION, (P, 1)), minus_half=np.full((P, 8), -0.5, f),
        q_rows=q_rows.astype(bf16), k_rows=k_rows.astype(bf16),
    )


def kernel(L0_attn_x, L0_attn_Wq, L0_attn_bq, L0_attn_Wkd, L0_attn_bkd, L0_attn_Wku, L0_attn_bku, L0_attn_Wo,
           L0_attn_bo, L0_ffn_g1, L0_ffn_be1, L0_ffn_mix_w, L0_ffn_mix_b, L0_ffn_g2, L0_ffn_be2, L0_ffn_router_w,
           L0_ffn_w1, L0_ffn_b1, L0_ffn_w2, L0_ffn_b2, L1_attn_Wq, L1_attn_Wk, L1_attn_Wv, L1_attn_Wo,
           L1_ffn_gate_w, L1_ffn_w1, L1_ffn_b1, L1_ffn_w2, L1_ffn_b2):
    import ml_dtypes
    import numpy as np
    import concourse.bacc as bacc
    from concourse.bass_utils import run_bass_kernel_spmd

    def a(v):
        return np.ascontiguousarray(np.asarray(v))

    wku, bku = a(L0_attn_Wku), a(L0_attn_bku)
    wku = np.concatenate([heads_apart(wku[:, :C], np), wku[:, C:]], axis=1)
    named = dict(
        wq0=heads_apart(L0_attn_Wq, np), wq1=heads_apart(a(L1_attn_Wq).T, np),
        wo0=a(L0_attn_Wo), wo1=a(a(L1_attn_Wo).T), router0=a(L0_ffn_router_w), router1=a(a(L1_ffn_gate_w).T),
        wkd=a(L0_attn_Wkd), wku=a(np.concatenate([wku, wku], axis=0)),
        wk1=heads_apart(a(L1_attn_Wk).T, np), wv1=a(a(L1_attn_Wv).T),
        bq=heads_apart(L0_attn_bq, np)[:, None], bk=heads_apart(bku[:C], np)[:, None], bkd=a(L0_attn_bkd)[:, None],
        mix=a(L0_ffn_mix_w), bv=a(bku[C:]), bo=a(L0_attn_bo), g1=a(L0_ffn_g1), be1=a(L0_ffn_be1),
        mix_b=a(L0_ffn_mix_b), g2=a(L0_ffn_g2), be2=a(L0_ffn_be2),
        e0_w1=a(L0_ffn_w1), e0_b1=by_partition(L0_ffn_b1, np), e0_w2=a(L0_ffn_w2), e0_b2=a(L0_ffn_b2),
        e1_w1=a(L1_ffn_w1), e1_b1=by_partition(L1_ffn_b1, np), e1_w2=a(L1_ffn_w2), e1_b2=a(L1_ffn_b2),
    )
    constants = shape_constants(np, ml_dtypes.bfloat16)
    arrays = {"x": a(L0_attn_x), **named, **constants}
    arrays = {name: a(v) for name, v in arrays.items()}
    nc = bacc.Bacc("TRN2", target_bir_lowering=False, num_devices=1)
    aps = {name: nc.dram_tensor("in_" + name, v.shape, mybir.dt.from_np(v.dtype), kind="ExternalInput").ap()
           for name, v in arrays.items()}
    out = nc.dram_tensor("out", (B, T, C), F32, kind="ExternalOutput").ap()
    weights = {name: aps[name] for name in named if name[:3] not in ("e0_", "e1_")}
    weights["experts"] = [[aps[f"e{layer}_{w}"] for w in ("w1", "b1", "w2", "b2")] for layer in range(2)]
    sandwich(nc, aps["x"], {name: aps[name] for name in constants}, weights, out)
    result = run_bass_kernel_spmd(nc, [{"in_" + name: v for name, v in arrays.items()}], core_ids=[0])
    return result.results[0]["out"]
```

```python
from contextlib import ExitStack
import concourse.bass as bass
from concourse import mybir

F32 = mybir.dt.float32
BF16 = mybir.dt.bfloat16
I32 = mybir.dt.int32
U32 = mybir.dt.uint32
ALU = mybir.AluOpType
ACT = mybir.ActivationFunctionType
AX = mybir.AxisListType.X

P = 128
B, T, C = 16, 512, 128
H, D = 16, 8
TT = T // P
PAIRS = H // 2
SCALE = D ** -0.5
EPS = 1e-5
NB = 3
TERMS = 6
ALIBI_ROW = TERMS * D
MAX_ROW = ALIBI_ROW + 3
SLOTS = TT * (H // 4)
GROUPS = 2 * SLOTS
MAX_GROUPS = [(qt, h0, n) for qt, n in ((0, 4), (1, 2), (2, 1), (3, 1)) for h0 in range(0, 8, n)]
MG = len(MAX_GROUPS)
MAX_PER_SLOT = [3, 3, 3, 3, 3, 3, 2, 2]
NEG = -1e30
LOADS = 16 * 4
WRITES = 16 * 3


def has(b):
    return not isinstance(b, int) or 0 <= b < B


def begun(count):
    return not isinstance(count, int) or count > 0


class Attention:

    def __init__(self, stack, ctx, nc, x_sb):
        def sb(name, shape, dt=F32):
            return stack.enter_context(nc.sbuf_tensor(name, shape, dt))

        def sem(name):
            return ctx.enter_context(nc.semaphore(name))

        self.x = x_sb
        self.q_stack = sb("q_stack", [P, NB, PAIRS, T], BF16)
        self.k_stack = sb("k_stack", [P, NB, 2, PAIRS, T], BF16)
        self.v_aug = sb("v_aug", [P, NB, TT, H, 32])
        self.probs = sb("probs", [P, 4, 2, T])
        self.xn = sb("xn", [P, TT, C])
        self.xn_t = sb("xn_t", [P, T])
        self.gelu = sb("gelu", [64, T])
        self.part = sb("part", [P, 2, 3, T], BF16)
        self.full = sb("full", [P, 2, T])
        self.rest = sb("rest", [P, T])
        self.neg_max = sb("neg_max", [P, 2, TT, 8])
        self.max_rest = sb("max_rest", [P, TT, 8])
        self.max_part = sb("max_part", [P, 2, TT, 3, 8], BF16)
        self.max_t = sb("max_t", [24, 2, T], BF16)
        self.quad = sb("quad", [P, T])
        self.recip = sb("recip", [P, TT, 4])
        self.heads_out = sb("heads_out", [P, TT, H, D])
        self.heads_t = sb("heads_t", [P, T])
        self.y = sb("y", [P, TT, C])
        self.stats = sb("stats", [P, 2, TT, 6])
        self.mean_var = sb("mean_var", [P, 2, TT, 2])
        self.rstd = sb("rstd", [P, 2, TT])
        (self.xn_stats, self.xn_var, self.xn_rstd, self.xn_ready, self.xnt_full, self.xnt_ready) = (sem(name) for name in
            "xn_stats xn_var xn_rstd xn_ready xnt_full xnt_ready".split())
        (self.gelu_full, self.gelu_ready, self.q_full, self.q_ready, self.k_full, self.k_ready) = (sem(name) for name in
            "gelu_full gelu_ready q_full q_ready k_full k_ready".split())
        (self.first_ready, self.rest_ready, self.mid_ready, self.parts_ready, self.v_full, self.v_ready,
         self.parts_written) = (sem(name) for name in
            "first_ready rest_ready mid_ready parts_ready v_full v_ready parts_written".split())
        (self.stack_loaded, self.max_full, self.max_taken, self.max_step, self.max_parts,
         self.maxt_full) = (sem(name) for name in
            "stack_loaded max_full max_taken max_step max_parts maxt_full".split())
        (self.maxt_ready, self.max_written, self.max_loaded, self.scores_full, self.probs_ready,
         self.pv_done) = (sem(name) for name in
            "maxt_ready max_written max_loaded scores_full probs_ready pv_done".split())
        (self.quad_ready, self.outt_full, self.out_recip, self.out_ready, self.headst_full,
         self.headst_ready) = (sem(name) for name in
            "quad_ready outt_full out_recip out_ready headst_full headst_ready".split())
        (self.y_full, self.y_ready, self.y_stats, self.y_var, self.y_rstd, self.y_normed) = (sem(name) for name in
            "y_full y_ready y_stats y_var y_rstd y_normed".split())
        (self.x_ready, self.xn_eps, self.y_eps, self.v_zeroed, self.v_set, self.rows_set, self.rows_written) = (sem(name) for name in
            "x_ready xn_eps y_eps v_zeroed v_set rows_set rows_written".split())


def max_schedule():
    order = [(ph, g) for ph in range(2) for g in range(MG)]
    out = []
    for n in MAX_PER_SLOT * 2:
        out.append(order[:n])
        order = order[n:]
    assert not order
    return out




def sweep(eng, body, first):
    lo, hi = 4, B - 3
    for n in range(first, lo):
        body(n, n % NB)
    with eng.Fori(0, (hi - lo) // NB) as i:
        for u in range(NB):
            body(i * NB + (lo + u), (lo + u) % NB)
    for n in range(hi, B + 3):
        body(n, n % NB)


def attention_tensor(pe, nc, A, W, R, Q=None):
    mm, tr = nc.tensor.matmul, nc.tensor.transpose
    layer = R.layer
    first = layer * B
    schedule = max_schedule()
    misc16 = W.misc[:, :].bitcast(BF16)

    def body(n, turn):
        now = n + first
        cur, nxt, new = turn, (turn + 1) % NB, (turn + 2) % NB
        if has(n - 1) and (not isinstance(n, int) or n >= 1):
            free = (A.out_ready, TT * now - 1)
        elif n > 0:
            free = (R.less_ready, n - 2)
        else:
            free = (A.v_ready, now + 2) if n > -2 else None

        def misc_is_free():
            if free:
                pe.wait_ge(*free)

        def scores(slot, half_of_quad):
            j, kt = divmod(slot, TT)
            pair, g = 2 * j + half_of_quad, 2 * slot + half_of_quad
            if slot == 0 and half_of_quad == 0:
                pe.wait_ge(A.max_loaded, 64 * now + 32)
            if slot == SLOTS // 2 and half_of_quad == 0:
                pe.wait_ge(A.max_loaded, 64 * now + 64)
            if begun(GROUPS * now + g - 1):
                pe.wait_ge(A.probs_ready, GROUPS * now + g - 1)
            for half in range(2):
                bank = W.s_ps[:, 2 * (g % 2) + half, :]
                mm(bank[:, 0:P], W.causal[:, :], W.ident16[:, :], start=True, stop=False,
                   skip_group_check=True)
                last = mm(bank[:, 0:T - kt * P],
                          A.k_stack[:, cur, half, pair, kt * P:(kt + 1) * P],
                          A.q_stack[:, cur, pair, kt * P:T], start=False, stop=True, skip_group_check=True)
            last.then_inc(A.scores_full, 1)

        def weigh(slot, at, buf):
            j, kt = divmod(slot, TT)
            if kt == 0:
                if begun(TT * at + j):
                    pe.wait_ge(A.quad_ready, TT * at + j)
            for i in range(2):
                g = 2 * slot + i
                pe.wait_ge(A.probs_ready, GROUPS * at + g + 1)
                for half in range(2):
                    c = 2 * i + half
                    last = mm(W.o_ps[32 * c:32 * c + 32, kt * P:T],
                              A.v_aug[:, buf, kt, 4 * j + c, :],
                              A.probs[:, g % 4, half, 0:T - kt * P],
                              start=(kt == 0), stop=(kt == TT - 1))
                last.then_inc(A.pv_done, 1)

        def max_group(ph, g):
            qt, h0, heads = MAX_GROUPS[g]
            if ph == 0 and g == 0:
                pe.wait_ge(A.stack_loaded, LOADS * (now + 2))
            count = 2 * MG * (now + 1) + ph * MG + g
            if begun(count - 1):
                pe.wait_ge(A.max_taken, count - 1)
            keys = (qt + 1) * P
            bank = W.m_ps[:, g % 2, 0:heads * keys].rearrange("p (h k) -> p h k", h=heads)
            mm(bank[:, :, keys - P:keys], W.ident16[:, :],
               W.causal[:, :].unsqueeze(1).to_broadcast([P, heads, P]), start=True, stop=False,
               skip_group_check=True)
            for h in range(h0, h0 + heads):
                half, pair = h // 4, 4 * ph + h % 4
                last = mm(bank[:, h - h0, :], A.q_stack[:, nxt, pair, qt * P:(qt + 1) * P],
                          A.k_stack[:, nxt, half, pair, 0:keys], start=False,
                          stop=(h == h0 + heads - 1), skip_group_check=True)
            last.then_inc(A.max_full, 1)

        def max_turned(ph, at):
            misc_is_free()
            pe.wait_ge(A.max_parts, 2 * at + ph + 1)
            for qt in range(TT):
                last = tr(misc16[0:24, qt * P:(qt + 1) * P],
                          A.max_part[:, ph, qt, :, :].rearrange("p a b -> p (a b)"), W.ident16[:, :])
            last.then_inc(A.maxt_full, 1)
            return A.maxt_ready, 2 * at + ph + 1

        def heads_turned(j, at):
            misc_is_free()
            pe.wait_ge(A.quad_ready, TT * at + j + 1)
            for t in range(TT):
                last = tr(W.misc[:, t * P:(t + 1) * P], A.quad[:, t * P:(t + 1) * P], W.ident[:, :])
            last.then_inc(A.outt_full, 1)
            return A.out_ready, TT * at + j + 1

        def project_x():
            misc_is_free()
            pe.wait_ge(A.xn_ready, now + 3)
            for t in range(TT):
                last = tr(W.misc[:, t * P:(t + 1) * P], A.xn[:, t, :], W.ident[:, :])
            last.then_inc(A.xnt_full, 1)
            return A.xnt_ready, now + 3

        def project_latent():
            misc_is_free()
            pe.wait_ge(A.xnt_ready, now + 3)
            mm(W.misc[0:64, :], W.wkd[:, :], A.xn_t[:, :], start=True, stop=True).then_inc(A.gelu_full, 1)
            return A.gelu_ready, now + 3

        def project_q():
            misc_is_free()
            pe.wait_ge(A.xnt_ready, now + 3)
            mm(W.misc[:, :], W.wq[layer][:, :], A.xn_t[:, :], start=True, stop=True).then_inc(A.q_full, 1)
            return A.q_ready, now + 3

        def project_k():
            misc_is_free()
            if layer == 0:
                pe.wait_ge(A.gelu_ready, now + 3)
                last = mm(W.misc[:, :], W.wku[:, 0:C], A.gelu[:, :], start=True, stop=True)
            else:
                last = mm(W.misc[:, :], W.wk1[:, :], A.xn_t[:, :], start=True, stop=True)
            last.then_inc(A.k_full, 1)
            return A.k_ready, now + 3

        def project_v():
            misc_is_free()
            for t in range(TT):
                rows = slice(t * P, (t + 1) * P)
                if layer == 0:
                    last = mm(W.misc[:, rows], A.gelu[:, rows], W.wku[:, C:2 * C], start=True, stop=True)
                else:
                    last = mm(W.misc[:, rows], A.xn_t[:, rows], W.wv1[:, :], start=True, stop=True)
            last.then_inc(A.v_full, 1)
            return A.v_ready, now + 3

        def finish_turned():
            misc_is_free()
            pe.wait_ge(A.out_ready, TT * now)
            for t in range(TT):
                last = tr(W.misc[:, t * P:(t + 1) * P],
                          A.heads_out[:, t, :, :].rearrange("p h d -> p (h d)"), W.ident[:, :])
            last.then_inc(A.headst_full, 1)
            return A.headst_ready, now

        def finish_y():
            misc_is_free()
            pe.wait_ge(A.headst_ready, now)
            for t in range(TT):
                rows = slice(t * P, (t + 1) * P)
                last = mm(W.misc[:, rows], A.heads_t[:, rows], W.wo[layer][:, :], start=True, stop=True)
            last.then_inc(A.y_full, 1)
            return A.y_ready, now

        for slot in range(SLOTS):
            groups = schedule[slot] if has(n + 1) else []
            if has(n):
                scores(slot, 0)
            for ph, g in groups[:1]:
                max_group(ph, g)
            if slot == 6 and has(n - 2) and layer == 0:
                misc_is_free()
                free = route_turn_n(pe, nc, R, W, n - 2)
            if slot == 8 and has(n - 2) and layer == 0:
                misc_is_free()
                free = route_mix(pe, nc, R, W, n - 2)
            if slot == 5 and has(n - 1):
                free = finish_turned()
            if has(n):
                scores(slot, 1)
            for ph, g in groups[1:2]:
                max_group(ph, g)
            if slot % TT == 1:
                for ph, g in groups[2:]:
                    max_group(ph, g)
            if slot == 0 and has(n - 1):
                weigh(SLOTS - 1, now - 1, (cur - 1) % NB)
            if slot > 0 and has(n):
                weigh(slot - 1, now, cur)
            if slot % TT != 1:
                for ph, g in groups[2:]:
                    max_group(ph, g)
            if slot == 0 and has(n):
                free = max_turned(1, now)
            if slot == 1 and has(n - 1):
                free = heads_turned(3, now - 1)
            if slot == 2 and has(n + 2):
                free = project_x()
            if slot == 3 and has(n + 2) and layer == 0:
                free = project_latent()
            if slot == 4 and has(n + 2):
                free = project_q()
            if slot == 5 and has(n + 2):
                free = project_k()
            if slot in (6, 10, 14) and has(n):
                free = heads_turned({6: 0, 10: 1, 14: 2}[slot], now)
            if slot == 7 and has(n - 3):
                misc_is_free()
                free = route_ranks(pe, nc, R, W, n - 3)
            if slot == 8 and has(n - 1):
                free = finish_y()
            if slot == 9 and has(n + 1):
                free = max_turned(0, now + 1)
            if slot == 11 and isinstance(n, int) and n == -2:
                pe.wait_ge(A.v_set, layer + 1)
            if slot == 11 and has(n + 2):
                free = project_v()
            if slot == 12 and has(n - 2):
                misc_is_free()
                free = route_turn_rows(pe, nc, R, W, n - 2, nxt)
            if slot == 13 and has(n - 2):
                misc_is_free()
                free = route_logits(pe, nc, R, W, n - 2)

    sweep(pe, body, -2 if layer == 0 else -3)


def attention_scalar(act, nc, A, W, R, Q=None):
    do = nc.scalar.activation
    layer = R.layer
    first = layer * B

    def body(n, turn):
        now = n + first

        def exps(slot, i):
            kt, g = slot % TT, 2 * slot + i
            act.wait_ge(A.scores_full, GROUPS * now + g + 1)
            if begun(GROUPS * now + g - 3):
                act.wait_ge(A.pv_done, GROUPS * now + g - 3)
            do(A.probs[:, g % 4, :, 0:T - kt * P], W.s_ps[:, 2 * (g % 2):2 * (g % 2) + 2, 0:T - kt * P],
               ACT.Exp, scale=SCALE).then_inc(A.probs_ready, 1)

        def take_quad(j, at):
            act.wait_ge(A.pv_done, GROUPS * at + 8 * (j + 1))
            if begun(TT * at + j):
                act.wait_ge(A.outt_full, TT * at + j)
            do(A.quad[:, :], W.o_ps[:, :], ACT.Copy).then_inc(A.quad_ready, 1)

        def take_turned_max(ph, at):
            act.wait_ge(A.maxt_full, 2 * at + ph + 1)
            if begun(16 * (2 * (at - 1) + ph + 1)):
                act.wait_ge(A.max_written, 16 * (2 * (at - 1) + ph + 1))
            do(A.max_t[:, ph, :], W.misc[0:24, 0:T // 2].bitcast(BF16), ACT.Copy).then_inc(A.maxt_ready, 1)

        def take_whole(which, bias, full, ready):
            act.wait_ge(full, now + 3)
            if begun(2 * (now + 2)):
                act.wait_ge(A.rest_ready, 2 * (now + 2))
            if bias is None:
                do(A.full[:, which, :], W.misc[:, :], ACT.Copy).then_inc(ready, 1)
            else:
                do(A.full[:, which, :], W.misc[:, :], ACT.Identity, bias=bias).then_inc(ready, 1)

        for slot in range(SLOTS):
            if slot == 1 and has(n):
                take_turned_max(1, now)
            if slot == 10 and has(n + 1):
                take_turned_max(0, now + 1)
            if slot == 9 and has(n - 1) and layer == 1:
                act.wait_ge(A.y_full, now)
                if begun(now - 1):
                    act.wait_ge(A.x_ready, now - 1)
                do(A.y[:, :, :].rearrange("p t c -> p (t c)"), W.misc[:, :], ACT.Copy).then_inc(A.y_ready, 1)
            if slot == 12 and has(n + 2) and layer == 1:
                act.wait_ge(A.v_full, now + 3)
                if begun(GROUPS * now):
                    act.wait_ge(A.pv_done, GROUPS * now)
                do(A.v_aug[:, (turn + 2) % NB, :, :, 0:D],
                   W.misc[:, :].rearrange("p (t h d) -> p t h d", t=TT, d=D), ACT.Copy).then_inc(A.v_ready, 1)
            if slot == 3 and has(n + 2):
                act.wait_ge(A.xnt_full, now + 3)
                if begun(now + 2):
                    act.wait_ge(A.v_full, now + 2)
                do(A.xn_t[:, :], W.misc[:, :], ACT.Copy).then_inc(A.xnt_ready, 1)
            if slot == 4 and has(n + 2) and layer == 0:
                act.wait_ge(A.gelu_full, now + 3)
                do(A.gelu[:, :], W.misc[0:64, :], ACT.Gelu, bias=W.bkd[:, :]).then_inc(A.gelu_ready, 1)
            if slot == 5 and has(n + 2):
                take_whole(0, W.bq[:, :] if layer == 0 else None, A.q_full, A.q_ready)
            if slot == 6 and has(n + 2):
                take_whole(1, W.bk[:, :] if layer == 0 else None, A.k_full, A.k_ready)
            if slot == 13 and has(n - 2):
                route_scalar_rows(act, nc, R, W, n - 2)
            if has(n):
                exps(slot, 0)
            if slot == 5 and has(n - 1):
                act.wait_ge(A.headst_full, now)
                do(A.heads_t[:, :], W.misc[:, :], ACT.Copy).then_inc(A.headst_ready, 1)
            if slot == 6 and has(n - 2) and layer == 0:
                route_scalar_n(act, nc, R, W, n - 2)
            if has(n):
                exps(slot, 1)
            if slot == 14 and has(n - 2):
                route_scalar_exp(act, nc, R, W, n - 2)
            if slot == 0 and has(n - 1):
                take_quad(3, now - 1)
            if slot in (4, 8, 12) and has(n):
                take_quad(slot // 4 - 1, now)

    sweep(act, body, -2 if layer == 0 else -3)


def attention_vector(dve, nc, A, W, R, Q=None):
    v = nc.vector
    layer = R.layer
    first = layer * B
    schedule = max_schedule()

    def body(n, turn):
        now = n + first
        cur, nxt, new = turn, (turn + 1) % NB, (turn + 2) % NB

        def take_max(ph, g):
            qt, h0, heads = MAX_GROUPS[g]
            if g == 0:
                if begun(2 * now + ph + 1):
                    dve.wait_ge(A.max_parts, 2 * now + ph + 1)
            dve.wait_ge(A.max_full, 2 * MG * (now + 1) + ph * MG + g + 1)
            v.tensor_reduce(A.neg_max[:, ph, qt, h0:h0 + heads],
                            W.m_ps[:, g % 2, 0:heads * (qt + 1) * P].rearrange("p (h k) -> p h k", h=heads),
                            AX.X, ALU.max, negate=True).then_inc(A.max_taken, 1)

        def split_max(ph):
            src, part, rest = A.neg_max[:, ph, :, :], A.max_part[:, ph], A.max_rest[:, :, :]
            steps = 3 * (2 * (now + 1) + ph)
            dve.wait_ge(A.max_taken, 2 * MG * (now + 1) + (ph + 1) * MG)
            if begun(2 * now + ph + 1):
                dve.wait_ge(A.maxt_full, 2 * now + ph + 1)
            v.tensor_copy(part[:, :, 0, :], src).then_inc(A.max_step, 1)
            dve.wait_ge(A.max_step, steps + 1)
            v.tensor_tensor(rest, src, part[:, :, 0, :], ALU.subtract).then_inc(A.max_step, 1)
            dve.wait_ge(A.max_step, steps + 2)
            v.tensor_copy(part[:, :, 1, :], rest).then_inc(A.max_step, 1)
            dve.wait_ge(A.max_step, steps + 3)
            v.tensor_tensor(part[:, :, 2, :], rest, part[:, :, 1, :], ALU.subtract).then_inc(A.max_parts, 1)

        def take_heads(j, at):
            quad = W.misc[:, :].rearrange("p (t h c) -> p t h c", t=TT, h=4)
            dve.wait_ge(A.outt_full, TT * at + j + 1)
            if j == 0:
                if begun(at):
                    dve.wait_ge(A.headst_full, at)
            v.reciprocal(A.recip[:, :, :], quad[:, :, :, D]).then_inc(A.out_recip, 1)
            dve.wait_ge(A.out_recip, TT * at + j + 1)
            v.tensor_tensor(A.heads_out[:, :, 4 * j:4 * j + 4, :], quad[:, :, :, 0:D],
                            A.recip[:, :, :].unsqueeze(3).to_broadcast([P, TT, 4, D]),
                            ALU.mult).then_inc(A.out_ready, 1)

        def mean_var(src, k, stats_sem, var_sem, count):
            for t in range(TT):
                last = v.bn_stats(A.stats[:, k, t, :], src(t))
            last.then_inc(stats_sem, 1)
            dve.wait_ge(stats_sem, count)
            dve.sem_inc(W.passed, 1)
            for t in range(TT):
                last = v.bn_aggr(A.mean_var[:, k, t, :], A.stats[:, k, t, :])
            last.then_inc(var_sem, 1)

        def normalise(dst, src, k, sem):
            for t in range(TT):
                last = v.tensor_scalar(dst[:, t, :], src(t), A.mean_var[:, k, t, 0:1],
                                       A.rstd[:, k, t:t + 1], ALU.subtract, ALU.mult)
            last.then_inc(sem, 1)

        def x_in(t):
            return A.x[:, (n + 2) * TT + t, :]

        for slot in range(SLOTS):
            if slot == 0 and has(n + 3) and layer == 1:
                collect_index(dve, nc, Q, n + 3, turn)
            groups = schedule[slot] if has(n + 1) else []
            for ph, g in groups[:1]:
                take_max(ph, g)
            if slot == 8 and has(n - 2) and layer == 0:
                route.mixed(n - 2)
            for ph, g in groups[1:]:
                take_max(ph, g)
            if slot == 14 and has(n - 2):
                route.logits(n - 2)
            if slot == 1 and has(n - 1):
                take_heads(3, now - 1)
            if slot == 0 and has(n + 2):
                W.wait_for_x(dve, layer, n + 2)
                if begun(now + 2):
                    dve.wait_ge(A.xn_rstd, now + 2)
                    dve.sem_inc(W.passed, 1)
                mean_var(x_in, 0, A.xn_stats, A.xn_var, now + 3)
            if slot == 1 and has(n + 2):
                dve.wait_ge(A.xn_rstd, now + 3)
                if begun(now + 2):
                    dve.wait_ge(A.xnt_full, now + 2)
                normalise(A.xn, x_in, 0, A.xn_ready)
            if slot in (6, 8) and has(n + 2):
                which = 0 if slot == 6 else 1
                dve.wait_ge(A.rest_ready, 2 * (now + 2) + which + 1)
                v.tensor_copy(A.part[:, which, 1, :], A.rest[:, :]).then_inc(A.mid_ready, 1)
            if slot == 8 and has(n - 1) and layer == 0:
                dve.wait_ge(A.y_full, now)
                if begun(now - 1):
                    dve.wait_ge(A.x_ready, now - 1)
                v.tensor_tensor(A.y[:, :, :], W.misc[:, :].rearrange("p (t c) -> p t c", t=TT),
                                W.bo[:, :].unsqueeze(1).to_broadcast([P, TT, C]), ALU.add).then_inc(A.y_ready, 1)
            if slot == 7 and has(n + 1):
                split_max(0)
            if slot in (6, 10, 14) and has(n):
                take_heads({6: 0, 10: 1, 14: 2}[slot], now)
            if slot == 11 and has(n + 2) and layer == 0:
                dve.wait_ge(A.v_full, now + 3)
                if begun(GROUPS * now):
                    dve.wait_ge(A.pv_done, GROUPS * now)
                v.tensor_tensor(A.v_aug[:, new, :, :, 0:D],
                                W.misc[:, :].rearrange("p (t h d) -> p t h d", t=TT, d=D),
                                W.bv[:, :].rearrange("p (h d) -> p h d", d=D).unsqueeze(1)
                                .to_broadcast([P, TT, H, D]), ALU.add).then_inc(A.v_ready, 1)
            if slot == 15 and has(n + 1):
                split_max(1)
            if slot == 7 and has(n - 3):
                route.take_ranks(n - 3)
            if slot == 1 and isinstance(n, int) and n == -2:
                v.memset(A.k_stack[64:P, :, 0, :, :].bitcast(F32), 0.0)
                v.memset(A.k_stack[0:64, :, 1, :, :].bitcast(F32), 0.0).then_inc(A.rows_set, 1)
            if slot == 2 and has(n - 2):
                route.x_stats(n - 2)
            if slot == 3 and has(n - 2):
                route.x_norm(n - 2, nxt)
            if slot == 4 and has(n - 2) and layer == 0:
                route.second_norm(n - 2)
            if slot == 5 and has(n - 3):
                route.choose(n - 3)
            if slot == 7 and has(n - 3):
                route.place(n - 3, cur)
            if slot == 8 and has(n - 2) and layer == 0:
                route.mixed_stats(n - 2)
            if slot == 9 and has(n - 2) and layer == 0:
                route.third_norm(n - 2)
            if slot == 9 and has(n - 1):
                dve.wait_ge(A.y_ready, now)
                mean_var(lambda t: A.y[:, t, :], 1, A.y_stats, A.y_var, now)
            if slot == 11 - layer and has(n - 1):
                dve.wait_ge(A.y_rstd, now)
                normalise(A.y, lambda t: A.y[:, t, :], 1, A.y_normed)
            if slot in (11, 13) and has(n + 3) and layer == 1:
                collect_sum(dve, nc, Q, W, n + 3, parts=((slot - 11) // 2,))
            if slot == 15 and has(n + 3) and layer == 1:
                collect_add(dve, nc, Q, A, n + 3)

    route = RouteVector(dve, nc, R, A, W)
    v.memset(R.seen[:, :], 0.0).then_inc(R.seen_ready, 1)
    sweep(dve, body, -2 if layer == 0 else -3)


def attention_gpsimd(pool, nc, A, W, R, Q=None):
    g_ = nc.gpsimd
    layer = R.layer
    first = layer * B

    def body(n, turn):
        now = n + first
        cur, nxt = turn, (turn + 1) % NB

        def rstd(k, var_sem, rstd_sem, count, step_sem):
            pool.wait_ge(var_sem, count)
            pool.sem_inc(W.passed, 1)
            g_.tensor_scalar(A.rstd[:, k, :], A.mean_var[:, k, :, 1], EPS, None, ALU.add).then_inc(step_sem, 1)
            pool.wait_ge(step_sem, count)
            g_.tensor_tensor(A.rstd[:, k, :], A.rstd[:, k, :], W.minus_half[:, 0:TT], ALU.pow).then_inc(rstd_sem, 1)

        def first_part(which, ready):
            pool.wait_ge(ready, now + 3)
            if begun(now + 2):
                pool.wait_ge(A.parts_written, 2 * WRITES * (now + 2))
                pool.sem_inc(W.passed, 1)
            g_.tensor_copy(A.part[:, which, 0, :], A.full[:, which, :]).then_inc(A.first_ready, 1)

        def rest(which):
            pool.wait_ge(A.first_ready, 2 * (now + 2) + which + 1)
            if begun(2 * (now + 2) + which):
                pool.wait_ge(A.parts_ready, 2 * (now + 2) + which)
            g_.tensor_tensor(A.rest[:, :], A.full[:, which, :], A.part[:, which, 0, :],
                             ALU.subtract).then_inc(A.rest_ready, 1)

        def last_part(which):
            pool.wait_ge(A.mid_ready, 2 * (now + 2) + which + 1)
            g_.tensor_tensor(A.part[:, which, 2, :], A.rest[:, :], A.part[:, which, 1, :],
                             ALU.subtract).then_inc(A.parts_ready, 1)

        for slot in range(SLOTS):
            if slot == 0 and has(n + 2):
                if begun(now + 2):
                    pool.wait_ge(A.xn_ready, now + 2)
                    pool.sem_inc(W.passed, 1)
                rstd(0, A.xn_var, A.xn_rstd, now + 3, A.xn_eps)
            if slot == 1 and isinstance(n, int) and n == -2:
                g_.memset(A.v_aug[:, :, :, :, :], 0.0).then_inc(A.v_zeroed, 1)
                pool.wait_ge(A.v_zeroed, layer + 1)
                g_.memset(A.v_aug[:, :, :, :, D:D + 1], 1.0).then_inc(A.v_set, 1)
            if slot == 10 - layer and has(n - 1):
                rstd(1, A.y_var, A.y_rstd, now, A.y_eps)
            if slot == 12 - layer and has(n - 1):
                pool.wait_ge(A.y_normed, now)
                rows = A.x[:, bass.ds((n - 1) * TT, TT), :]
                g_.tensor_tensor(rows, rows, A.y[:, :, :], ALU.add).then_inc(A.x_ready, 1)
            if has(n - 2) and layer == 0:
                for step in {4: (0,), 5: (1,), 6: (2, 3), 10: (4,), 11: (5,)}.get(slot, ()):
                    route_gpsimd_scale(pool, nc, R, W, n - 2, nxt, step)
            if slot == 5 and has(n + 2):
                first_part(0, A.q_ready)
                rest(0)
            if slot == 7 and has(n + 2):
                last_part(0)
                first_part(1, A.k_ready)
                rest(1)
            if slot == 9 and has(n + 2):
                last_part(1)
            if slot == 2 and has(n - 2):
                route_gpsimd_rstd(pool, nc, R, W, R.norms * (n - 2) + 1)
            if slot == 3 and has(n - 2) and layer == 0:
                route_gpsimd_rstd(pool, nc, R, W, R.norms * (n - 2) + 2)
            if slot == 8 and has(n - 2) and layer == 0:
                route_gpsimd_rstd(pool, nc, R, W, R.norms * (n - 2) + 3)
            if slot >= 8 and has(n - 3):
                scatter(pool, nc, R, W, n - 3, cur, slot - 8)
            if 1 <= slot <= 8 and has(n + 3) and layer == 1:
                gather(pool, nc, Q, W, n + 3, turn, slot - 1)
            if slot == 13 and has(n + 3) and layer == 1:
                collect_rstd(pool, nc, Q, W, n + 3)

    sweep(pool, body, -2 if layer == 0 else -3)


def attention_sync(sp, nc, A, W, R, Q, X):
    layer = R.layer
    first = layer * B
    wide = PAIRS * T

    def body(n, turn):
        now = n + first
        cur, nxt, new = turn, (turn + 1) % NB, (turn + 2) % NB

        def maxima(ph, at, buf):
            sp.wait_ge(A.maxt_ready, 2 * at + ph + 1)
            sp.sem_inc(W.passed, 1)
            if begun(32 * (2 * at + ph)):
                sp.wait_ge(A.max_loaded, 32 * (2 * at + ph))
                sp.sem_inc(W.passed, 1)
            sp.dma_start(W.max_dram[ph], A.max_t[:, ph, :]).then_inc(A.max_written, 16)
            sp.wait_ge(A.max_written, 16 * (2 * at + ph + 1))
            sp.sem_inc(W.passed, 1)
            for half in range(2):
                sp.dma_start(
                    A.q_stack[64 * half + MAX_ROW:64 * half + MAX_ROW + 3, buf, 4 * ph:4 * ph + 4, :],
                    W.max_dram[ph].rearrange("(s h p) t -> h s p t", s=3, h=2)[half],
                ).then_inc(A.max_loaded, 16)

        def write_parts(which):
            sp.wait_ge(A.parts_ready, 2 * (now + 2) + which + 1)
            sp.sem_inc(W.passed, 1)
            term = 0
            for k in range(3):
                rows = W.stack_dram[which, term * D:(term + 3 - k) * D, :, :, :]
                if which == 0:
                    src = A.part[:, 0, 0:3 - k, :]
                else:
                    src = A.part[:, 1, k:k + 1, :].to_broadcast([P, 3 - k, T])
                sp.dma_start(rows.rearrange("(s d) h p t -> (d h p) s t", d=D), src).then_inc(A.parts_written, 16)
                term += 3 - k

        if isinstance(n, int) and n == B + 1:
            sp.wait_ge(A.scores_full, GROUPS * (first + B))
            load_weights(sp, nc, R, X, W)
        if has(n + 3) and layer == 1:
            collect_load(sp, Q, W, n + 3)
        if has(n):
            maxima(1, now, cur)
        if has(n - 2):
            b, src = n - 2, R.total[:, :, :] if layer == 0 else R.rows[:, nxt, :, :]
            if layer == 1:
                sp.wait_ge(R.rows_ready, b + 1)
                sp.sem_inc(W.passed, 1)
                sp.dma_start(W.kept[b].rearrange("(t p) c -> p t c", p=P), src).then_inc(R.kept_written, 16)
        if has(n + 2) and begun(LOADS * (now + 2)):
            sp.wait_ge(A.stack_loaded, LOADS * (now + 2))
            sp.sem_inc(W.passed, 1)
        if has(n + 2):
            write_parts(0)
        if has(n - 2) and layer == 0:
            sp.wait_ge(R.sum_ready, b + 1)
            sp.sem_inc(W.passed, 1)
            sp.dma_start(W.kept[b].rearrange("(t p) c -> p t c", p=P), src).then_inc(R.kept_written, 16)
        if has(n + 2):
            write_parts(1)
        if has(n + 1):
            maxima(0, now + 1, nxt)
        if has(n + 2):
            sp.wait_ge(A.parts_written, 2 * WRITES * (now + 3))
            sp.sem_inc(W.passed, 1)
            if begun(GROUPS * now):
                sp.wait_ge(A.scores_full, GROUPS * now)
                sp.sem_inc(W.passed, 1)
            if isinstance(n, int) and n == -2:
                sp.wait_ge(A.rows_set, layer + 1)
            for half in range(2):
                rows = slice(64 * half, 64 * half + 64)
                sp.dma_start(A.q_stack[rows, new, :, :], W.stack_dram[0, :, half]).then_inc(A.stack_loaded, 16)
                sp.dma_start(A.k_stack[rows, new, half, :, :], W.stack_dram[1, :, half]).then_inc(A.stack_loaded, 16)

    sp.dma_start(W.sorted_in[R.n * REGION:R.n * REGION + R.n * P, :].rearrange("(e p) c -> p e c", p=P),
                 spread(W.zeros[:, :], 1, [P, R.n, C])).then_inc(R.zeroed, 16)
    if begun(first):
        sp.wait_ge(A.x_ready, first)
        sp.sem_inc(W.passed, 1)
    sp.dma_start(W.stack_dram[0, ALIBI_ROW:64], W.q_rows).then_inc(A.rows_written, 16)
    sp.dma_start(W.stack_dram[1, ALIBI_ROW:64], W.k_rows[layer]).then_inc(A.rows_written, 16)
    sp.wait_ge(A.rows_written, 32 * (layer + 1))
    sp.sem_inc(W.passed, 1)
    sweep(sp, body, -2 if layer == 0 else -3)



TOP = 2
TILES = B * TT
REGION = B * T + P
MOVES = 16 * TT * TOP
MAX_E = 14


class Routing:

    def __init__(self, ctx, nc, bufs, layer, experts, width, table_steps, earlier_loads):
        self.layer, self.n, self.width = layer, experts, width
        self.table_start, self.table_steps = table_steps, table_steps + 12 + 2 * (experts - 1)
        self.chunks = width // P
        self.slots = TOP * TILES + experts
        self.weights_loads = 16 * (experts + 3) + earlier_loads
        self.norms = 3 if layer == 0 else 1
        def sb(name, shape):
            return ctx.enter_context(nc.sbuf_tensor(f"{name}{layer}", shape, F32))

        def sem(name):
            return ctx.enter_context(nc.semaphore(f"r{layer}_{name}"))

        (self.normed, self.second, self.total, self.got, self.kept, self.rows) = (bufs[name] for name in
            "normed second total got kept rows".split())
        (self.turned, self.stats, self.mean_var, self.rstd, self.neg_top, self.prob) = (bufs[name] for name in
            "turned stats mean_var rstd neg_top prob".split())
        (self.sum, self.best, self.best_at, self.best_f, self.hot, self.chosen) = (bufs[name] for name in
            "sum best best_at best_f hot chosen".split())
        (self.seen, self.new, self.rank, self.hot_rank, self.row_f, self.row) = (bufs[name] for name in
            "seen new rank hot_rank row_f row".split())
        (self.got_row, self.got_stats, self.got_mean_var, self.got_rstd, self.gap_i, self.gap) = (bufs[name] for name in
            "got_row got_stats got_mean_var got_rstd gap_i gap".split())
        (self.shift, self.tiles, self.tiles_i, self.marks, self.table_f, self.table) = (bufs[name] for name in
            "shift tiles tiles_i marks table_f table".split())
        (self.pad_row, self.passed, self.table_step, self.counts_full, self.tiles_ready,
         self.cum_full) = (bufs[name] for name in
            "pad_row passed table_step counts_full tiles_ready cum_full".split())
        (self.marks_ready, self.table_full, self.table_ready, self.pad_ready) = (bufs[name] for name in
            "marks_ready table_full table_ready pad_ready".split())
        self.row_all, self.weight = (sb(name, [P, TILES, TOP]) for name in ("row_all", "weight"))
        (self.place_step, self.choice_step, self.var, self.rstd_ready, self.eps_added, self.step, self.rows_ready) = (sem(name) for name in
            "place_step choice_step var rstd_ready eps_added step rows_ready".split())
        (self.ft_full, self.ft_ready, self.logits_full, self.less_ready, self.exp_ready,
         self.chosen_ready) = (sem(name) for name in
            "ft_full ft_ready logits_full less_ready exp_ready chosen_ready".split())
        (self.ranks_full, self.ranks_taken, self.row_ready, self.seen_ready, self.scattered,
         self.kept_written) = (sem(name) for name in
            "ranks_full ranks_taken row_ready seen_ready scattered kept_written".split())
        (self.index_ready, self.got_step, self.got_var, self.got_eps, self.got_rstd_ready,
         self.x_collected) = (sem(name) for name in
            "index_ready got_step got_var got_eps got_rstd_ready x_collected".split())
        (self.padded, self.zeroed) = (sem(name) for name in
            "padded zeroed".split())
        if layer == 0:
            (self.second_ready, self.n_ready, self.n_step, self.total_step, self.total_ready,
             self.nt_full) = (sem(name) for name in
                "second_ready n_ready n_step total_step total_ready nt_full".split())
            (self.nt_ready, self.mix_full, self.sum_ready, self.rows_step) = (sem(name) for name in
                "nt_ready mix_full sum_ready rows_step".split())
        self.gathered = [ctx.enter_context(nc.semaphore(f"r{layer}_gathered{i}")) for i in range(layer + 1)]
        self.kept_loaded = [ctx.enter_context(nc.semaphore(f"r{layer}_kept_loaded{i}")) for i in range(layer + 1)]


def table_events(ctx, nc):
    names = "table_step counts_full tiles_ready cum_full marks_ready table_full table_ready pad_ready"
    return {name: ctx.enter_context(nc.semaphore("r_" + name)) for name in names.split()}


def routing_buffers(ctx, nc):
    def sb(name, shape, dt=F32):
        return ctx.enter_context(nc.sbuf_tensor("route_" + name, shape, dt))

    shared = sb("shared", [P, TT * (TOP + 1), C])
    return dict(
        normed=shared[:, 0:TT, :], second=shared[:, TT:2 * TT, :], total=shared[:, 2 * TT:3 * TT, :],
        got=[shared[:, 0:2 * TT, :].rearrange("p (t j) c -> p t j c", j=TOP)], kept=[shared[:, 2 * TT:3 * TT, :]],
        rows=sb("rows", [P, NB, TT, C]), turned=sb("turned", [P, T]),
        stats=sb("stats", [P, TT, 6]), mean_var=sb("mean_var", [P, TT, 2]), rstd=sb("rstd", [P, TT]),
        neg_top=sb("neg_top", [P, TT]), prob=sb("prob", [P, TT, MAX_E]), sum=sb("sum", [P, TT]),
        best=sb("best", [P, TT, 8]), best_at=sb("best_at", [P, TT, 8], U32), best_f=sb("best_f", [P, TT, TOP]),
        hot=sb("hot", [P, TT, TOP, MAX_E]), chosen=sb("chosen", [P, TT, MAX_E], BF16),
        seen=sb("seen", [P, MAX_E], BF16), new=sb("new", [P, MAX_E]), rank=sb("rank", [P, TT, MAX_E]),
        hot_rank=sb("hot_rank", [P, TT, TOP, MAX_E]), row_f=sb("row_f", [P, TT, TOP]),
        row=sb("row", [P, NB, TT, TOP], U32), got_row=sb("got_row", [P, NB, TT, TOP], U32),
        
        got_stats=sb("got_stats", [P, TT, 6]), got_mean_var=sb("got_mean_var", [P, TT, 2]),
        got_rstd=sb("got_rstd", [P, TT]),
        gap_i=sb("gap_i", [P, 2, MAX_E], I32), gap=sb("gap", [P, MAX_E]), shift=sb("shift", [P, TILES * TOP]),
        tiles=sb("tiles", [MAX_E, 4]), tiles_i=sb("tiles_i", [MAX_E, 2], I32),
        marks=sb("marks", [MAX_E, TOP * TILES + MAX_E]), table_f=sb("table_f", [1, 2, TOP * TILES + MAX_E]),
        table=sb("table", [1, 2, TOP * TILES + MAX_E], I32), pad_row=sb("pad_row", [P, MAX_E], U32),
    )


def spread(ap, axis, shape):
    return ap.unsqueeze(axis).to_broadcast(shape)


def tiles_mean_var(dve, nc, R, src, stats, mean_var, step_sem, count, var_sem):
    for t in range(TT):
        last = nc.vector.bn_stats(stats[:, t, :], src(t))
    last.then_inc(step_sem, 1)
    dve.wait_ge(step_sem, count)
    dve.sem_inc(R.passed, 1)
    for t in range(TT):
        last = nc.vector.bn_aggr(mean_var[:, t, :], stats[:, t, :])
    last.then_inc(var_sem, 1)


def tiles_normalise(nc, dst, src, mean_var, rstd):
    for t in range(TT):
        last = nc.vector.tensor_scalar(dst(t), src(t), mean_var[:, t, 0:1], rstd[:, t:t + 1],
                                       ALU.subtract, ALU.mult)
    return last


class RouteVector:

    STEPS = (4, 1)
    CHOICE_STEPS = (8, 11)

    def __init__(self, dve, nc, R, A, W):
        self.dve, self.nc, self.R, self.A, self.W = dve, nc, R, A, W

    def stats(self, src, count):
        R = self.R
        tiles_mean_var(self.dve, self.nc, R, src, R.stats, R.mean_var, R.step, count, R.var)

    def x_stats(self, b):
        dve, R, A = self.dve, self.R, self.A
        dve.wait_ge(A.x_ready, b + 1 + R.layer * B)
        dve.sem_inc(R.passed, 1)
        self.stats(lambda t: A.x[:, b * TT + t, :], self.STEPS[R.layer] * b + 1)

    def x_norm(self, b, turn):
        dve, nc, R, A = self.dve, self.nc, self.R, self.A
        x = lambda t: A.x[:, b * TT + t, :]
        dve.wait_ge(R.rstd_ready, R.norms * b + 1)
        if R.layer == 1:
            if begun(16 * b):
                dve.wait_ge(R.kept_written, 16 * b)
            tiles_normalise(nc, lambda t: R.rows[:, turn, t, :], x, R.mean_var, R.rstd).then_inc(R.rows_ready, 1)
            return
        if begun(b):
            dve.wait_ge(R.total_ready, b)
        step = self.STEPS[0] * b + 1
        tiles_normalise(nc, lambda t: R.normed[:, t, :], x, R.mean_var, R.rstd).then_inc(R.step, 1)
        dve.wait_ge(R.step, step + 1)
        self.stats(lambda t: R.normed[:, t, :], step + 2)

    def second_norm(self, b):
        dve, nc, R = self.dve, self.nc, self.R
        dve.wait_ge(R.rstd_ready, 3 * b + 2)
        if begun(b):
            dve.wait_ge(R.rows_ready, b)
        tiles_normalise(nc, lambda t: R.second[:, t, :], lambda t: R.normed[:, t, :],
                        R.mean_var, R.rstd).then_inc(R.second_ready, 1)

    def mixed(self, b):
        dve, nc, R, W = self.dve, self.nc, self.R, self.W
        dve.wait_ge(R.mix_full, b + 1)
        dve.wait_ge(R.total_ready, b + 1)
        nc.vector.tensor_tensor(R.total[:, :, :], W.misc[:, :].rearrange("p (t c) -> p t c", t=TT),
                                R.total[:, :, :], ALU.add).then_inc(R.sum_ready, 1)

    def mixed_stats(self, b):
        dve, R = self.dve, self.R
        dve.wait_ge(R.sum_ready, b + 1)
        dve.sem_inc(R.passed, 1)
        self.stats(lambda t: R.total[:, t, :], self.STEPS[0] * b + 4)

    def third_norm(self, b):
        dve, nc, R = self.dve, self.nc, self.R
        dve.wait_ge(R.rstd_ready, 3 * b + 3)
        dve.wait_ge(R.nt_full, b + 1)
        tiles_normalise(nc, lambda t: R.second[:, t, :], lambda t: R.total[:, t, :],
                        R.mean_var, R.rstd).then_inc(R.second_ready, 1)

    def logits(self, b):
        dve, nc, R, W = self.dve, self.nc, self.R, self.W
        E = R.n
        step = self.CHOICE_STEPS[R.layer] * b
        logits = W.misc[:, 0:TT * E].rearrange("p (t e) -> p t e", t=TT)
        dve.wait_ge(R.logits_full, b + 1)
        nc.vector.tensor_reduce(R.neg_top[:, :], logits, AX.X, ALU.max, negate=True).then_inc(R.choice_step, 1)
        dve.wait_ge(R.choice_step, step + 1)
        nc.vector.tensor_tensor(R.prob[:, :, 0:E], logits, spread(R.neg_top[:, :], 2, [P, TT, E]),
                                ALU.add).then_inc(R.less_ready, 1)

    def choose(self, b):
        dve, nc, R = self.dve, self.nc, self.R
        v, E = nc.vector, R.n
        step = self.CHOICE_STEPS[R.layer] * b + 1
        prob = R.prob[:, :, 0:E]
        dve.wait_ge(R.exp_ready, b + 1)
        v.tensor_reduce(R.sum[:, :], prob, AX.X, ALU.add).then_inc(R.choice_step, 1)
        dve.wait_ge(R.choice_step, step + 1)
        v.reciprocal(R.sum[:, :], R.sum[:, :]).then_inc(R.choice_step, 1)
        dve.wait_ge(R.choice_step, step + 2)
        v.tensor_tensor(prob, prob, spread(R.sum[:, :], 2, [P, TT, E]), ALU.mult).then_inc(R.choice_step, 1)
        dve.wait_ge(R.choice_step, step + 3)
        dve.sem_inc(R.passed, 1)
        for t in range(TT):
            last = v.max(R.best[:, t, :], R.prob[:, t, 0:E])
        last.then_inc(R.choice_step, 1)
        dve.wait_ge(R.choice_step, step + 4)
        dve.sem_inc(R.passed, 1)
        for t in range(TT):
            last = v.max_index(R.best_at[:, t, :], R.best[:, t, :], R.prob[:, t, 0:E])
        last.then_inc(R.choice_step, 1)
        dve.wait_ge(R.choice_step, step + 5)
        v.tensor_copy(R.best_f[:, :, :], R.best_at[:, :, 0:TOP]).then_inc(R.choice_step, 1)
        dve.wait_ge(R.choice_step, step + 6)
        v.tensor_tensor(R.hot[:, :, :, 0:E],
                        self.W.numbers[:, 0:E].unsqueeze(1).unsqueeze(1).to_broadcast([P, TT, TOP, E]),
                        spread(R.best_f[:, :, :], 3, [P, TT, TOP, E]), ALU.is_equal).then_inc(R.choice_step, 1)
        dve.wait_ge(R.choice_step, step + 7)
        v.tensor_tensor(R.chosen[:, :, 0:E], R.hot[:, :, 0, 0:E], R.hot[:, :, 1, 0:E],
                        ALU.add).then_inc(R.chosen_ready, 1)
        best = R.best[:, :, 0:TOP]
        weight = R.weight[:, bass.ds(b * TT, TT), :]
        if R.layer == 0:
            v.tensor_copy(weight, best)
        else:
            v.tensor_tensor(R.sum[:, :], R.best[:, :, 0], R.best[:, :, 1], ALU.add).then_inc(R.choice_step, 1)
            dve.wait_ge(R.choice_step, step + 8)
            v.tensor_scalar(R.sum[:, :], R.sum[:, :], 1e-10, None, ALU.max).then_inc(R.choice_step, 1)
            dve.wait_ge(R.choice_step, step + 9)
            v.reciprocal(R.sum[:, :], R.sum[:, :]).then_inc(R.choice_step, 1)
            dve.wait_ge(R.choice_step, step + 10)
            v.tensor_tensor(weight, best, spread(R.sum[:, :], 2, [P, TT, TOP]), ALU.mult)

    def take_ranks(self, b):
        dve, nc, R, W = self.dve, self.nc, self.R, self.W
        v, E = nc.vector, R.n
        ranks = W.misc[:, 0:TT * E].rearrange("p (t e) -> p t e", t=TT)
        dve.wait_ge(R.ranks_full, b + 1)
        v.tensor_tensor(R.rank[:, :, 0:E], ranks, spread(W.regions[:, 0:E], 1, [P, TT, E]),
                        ALU.add).then_inc(R.ranks_taken, 1)

    def place(self, b, turn):
        dve, nc, R, W = self.dve, self.nc, self.R, self.W
        v, E = nc.vector, R.n
        step = 4 * b
        dve.wait_ge(R.ranks_taken, b + 1)
        v.tensor_tensor(R.hot_rank[:, :, :, 0:E], R.hot[:, :, :, 0:E],
                        spread(R.rank[:, :, 0:E], 2, [P, TT, TOP, E]), ALU.mult).then_inc(R.place_step, 1)
        dve.wait_ge(R.place_step, step + 1)
        v.tensor_reduce(R.row_f[:, :, :], R.hot_rank[:, :, :, 0:E], AX.X, ALU.add).then_inc(R.place_step, 1)
        dve.wait_ge(R.place_step, step + 2)
        if begun(MOVES * b):
            dve.wait_ge(R.scattered, MOVES * b)
        v.tensor_copy(R.row[:, turn, :, :], R.row_f[:, :, :]).then_inc(R.row_ready, 1)
        v.tensor_copy(R.row_all[:, bass.ds(b * TT, TT), :], R.row_f[:, :, :]).then_inc(R.place_step, 1)
        dve.wait_ge(R.place_step, step + 3)
        v.tensor_reduce(R.new[:, 0:E], R.chosen[:, :, 0:E].rearrange("p t e -> p e t"), AX.X, ALU.add).then_inc(R.place_step, 1)
        dve.wait_ge(R.place_step, step + 4)
        v.tensor_tensor(R.seen[:, 0:E], R.seen[:, 0:E], R.new[:, 0:E], ALU.add).then_inc(R.seen_ready, 1)


def route_gpsimd_rstd(pool, nc, R, W, count):
    pool.wait_ge(R.var, count)
    pool.sem_inc(W.passed, 1)
    nc.gpsimd.tensor_scalar(R.rstd[:, :], R.mean_var[:, :, 1], EPS, None, ALU.add).then_inc(R.eps_added, 1)
    pool.wait_ge(R.eps_added, count)
    nc.gpsimd.tensor_tensor(R.rstd[:, :], R.rstd[:, :], W.minus_half[:, 0:TT], ALU.pow).then_inc(R.rstd_ready, 1)


def route_gpsimd_scale(pool, nc, R, W, b, turn, step):
    def do(out, a, c, op, sem):
        nc.gpsimd.tensor_tensor(out, a, c, op).then_inc(sem, 1)

    row = lambda v: spread(v[:, :], 1, [P, TT, C])
    second, total = R.second[:, :, :], R.total[:, :, :]
    if step == 0:
        pool.wait_ge(R.second_ready, 2 * b + 1)
        do(second, second, row(W.g1), ALU.mult, R.n_step)
    elif step == 1:
        pool.wait_ge(R.n_step, b + 1)
        do(second, second, row(W.be1), ALU.add, R.n_ready)
    elif step == 2:
        pool.wait_ge(R.n_ready, b + 1)
        if begun(16 * b):
            pool.wait_ge(R.kept_written, 16 * b)
        do(total, R.normed[:, :, :], second, ALU.add, R.total_step)
    elif step == 3:
        pool.wait_ge(R.total_step, b + 1)
        do(total, total, row(W.mix_b), ALU.add, R.total_ready)
    elif step == 4:
        pool.wait_ge(R.second_ready, 2 * b + 2)
        do(second, second, row(W.g2), ALU.mult, R.rows_step)
    else:
        pool.wait_ge(R.rows_step, b + 1)
        do(R.rows[:, turn, :, :], second, row(W.be2), ALU.add, R.rows_ready)


def route_turn_n(pe, nc, R, W, b):
    pe.wait_ge(R.n_ready, b + 1)
    for t in range(TT):
        last = nc.tensor.transpose(W.misc[:, t * P:(t + 1) * P], R.second[:, t, :], W.ident[:, :])
    last.then_inc(R.nt_full, 1)
    return R.nt_ready, b + 1


def route_mix(pe, nc, R, W, b):
    pe.wait_ge(R.nt_ready, b + 1)
    for t in range(TT):
        rows = slice(t * P, (t + 1) * P)
        last = nc.tensor.matmul(W.misc[:, rows], R.turned[:, rows], W.mix[:, :], start=True, stop=True)
    last.then_inc(R.mix_full, 1)
    return R.sum_ready, b + 1


def route_turn_rows(pe, nc, R, W, b, turn):
    pe.wait_ge(R.rows_ready, b + 1)
    for t in range(TT):
        last = nc.tensor.transpose(W.misc[:, t * P:(t + 1) * P], R.rows[:, turn, t, :], W.ident[:, :])
    last.then_inc(R.ft_full, 1)
    return R.ft_ready, b + 1


def route_logits(pe, nc, R, W, b):
    E = R.n
    pe.wait_ge(R.ft_ready, b + 1)
    for t in range(TT):
        last = nc.tensor.matmul(W.misc[:, t * E:(t + 1) * E], R.turned[:, t * P:(t + 1) * P],
                                W.router[R.layer][:, :], start=True, stop=True)
    last.then_inc(R.logits_full, 1)
    return R.less_ready, b + 1


def route_ranks(pe, nc, R, W, b):
    mm, E = nc.tensor.matmul, R.n
    pe.wait_ge(R.chosen_ready, b + 1)
    pe.wait_ge(R.seen_ready, b + 1)
    ranks = W.misc[:, 0:TT * E].rearrange("p (t e) -> p t e", t=TT)
    mm(ranks, W.before[:, :], R.chosen[:, :, 0:E], start=True, stop=False, skip_group_check=True)
    for t in range(TT - 1):
        mm(ranks[:, t + 1:TT, :], W.ones16[:, :], spread(R.chosen[:, t, 0:E], 1, [P, TT - 1 - t, E]),
           start=False, stop=False, skip_group_check=True)
    mm(ranks, W.ones16[:, :], spread(R.seen[:, 0:E], 1, [P, TT, E]), start=False, stop=True,
       skip_group_check=True).then_inc(R.ranks_full, 1)
    return R.ranks_taken, b + 1


def route_scalar_n(act, nc, R, W, b):
    act.wait_ge(R.nt_full, b + 1)
    if begun(b):
        act.wait_ge(R.logits_full, b)
    nc.scalar.activation(R.turned[:, :], W.misc[:, :], ACT.Copy).then_inc(R.nt_ready, 1)


def route_scalar_rows(act, nc, R, W, b):
    act.wait_ge(R.ft_full, b + 1)
    if begun(b):
        act.wait_ge(R.logits_full, b)
    if R.layer == 0:
        act.wait_ge(R.mix_full, b + 1)
    nc.scalar.activation(R.turned[:, :], W.misc[:, :], ACT.Copy).then_inc(R.ft_ready, 1)


def route_scalar_exp(act, nc, R, W, b):
    act.wait_ge(R.less_ready, b + 1)
    prob = R.prob[:, :, 0:R.n]
    nc.scalar.activation(prob, prob, ACT.Exp).then_inc(R.exp_ready, 1)


def scatter(pool, nc, R, W, b, turn, k):
    t, j = divmod(k, TOP)
    if k == 0:
        pool.wait_ge(R.row_ready, b + 1)
        pool.sem_inc(W.passed, 1)
        pool.wait_ge(R.rows_ready, b + 1)
        pool.sem_inc(W.passed, 1)
    pool.indirect_dma_start(W.sorted_in, bass.IndirectOffsetOnAxis(ap=R.row[:, turn, t, j:j + 1], axis=0),
                            R.rows[:, turn, t, :], None).then_inc(R.scattered, 16)


def gather(pool, nc, R, W, b, turn, k, buf=0, bufs=1):
    t, j = divmod(k, TOP)
    if k == 0:
        pool.wait_ge(R.index_ready, b + 1)
        pool.sem_inc(W.passed, 1)
        if begun(b + 1 - bufs):
            pool.wait_ge(R.got_var, b + 1 - bufs)
            pool.sem_inc(W.passed, 1)
    pool.indirect_dma_start(R.got[buf][:, t, j, :], None, W.sorted_out[0:R.slots * P, :],
                            bass.IndirectOffsetOnAxis(ap=R.got_row[:, turn, t, j:j + 1], axis=0)
                            ).then_inc(R.gathered[buf], 16)


def collect_index(dve, nc, R, b, turn):
    nc.vector.tensor_copy(R.got_row[:, turn, :, :], R.row_all[:, bass.ds(b * TT, TT), :]).then_inc(R.index_ready, 1)


COLLECT_STEPS = 4


def collect_sum(dve, nc, R, W, b, buf=0, use=None, parts=(0, 1)):
    v = nc.vector
    got, kept = R.got[buf], R.kept[buf]
    step = (COLLECT_STEPS + R.layer) * b
    use = b if use is None else use
    if parts[0] == 0:
        dve.wait_ge(R.gathered[buf], MOVES * (use + 1))
        dve.wait_ge(R.kept_loaded[buf], 16 * (use + 1))
    for j in parts:
        for t in range(TT):
            last = v.scalar_tensor_tensor(kept[:, t, :], got[:, t, j, :], R.weight[:, b * TT + t, j:j + 1],
                                          kept[:, t, :], ALU.mult, ALU.add)
        last.then_inc(R.got_step, 1)
        dve.wait_ge(R.got_step, step + 1 + j)
    if parts[-1] < TOP - 1:
        return
    if R.layer == 1:
        v.tensor_scalar(kept[:, :, :], kept[:, :, :], 100.0, -100.0, ALU.min, ALU.max).then_inc(R.got_step, 1)
        dve.wait_ge(R.got_step, step + TOP + 1)
    tiles_mean_var(dve, nc, R, lambda t: kept[:, t, :], R.got_stats, R.got_mean_var, R.got_step,
                   step + TOP + 1 + R.layer, R.got_var)


def collect_add(dve, nc, R, A, b, buf=0):
    step = (COLLECT_STEPS + R.layer) * b + 3 + R.layer
    kept = lambda t: R.kept[buf][:, t, :]
    dve.wait_ge(R.got_rstd_ready, b + 1)
    tiles_normalise(nc, kept, kept, R.got_mean_var, R.got_rstd).then_inc(R.got_step, 1)
    dve.wait_ge(R.got_step, step + 1)
    rows = A.x[:, bass.ds(b * TT, TT), :]
    nc.vector.tensor_tensor(rows, rows, R.kept[buf][:, :, :], ALU.add).then_inc(R.x_collected, 1)


def collect_rstd(pool, nc, R, W, b):
    pool.wait_ge(R.got_var, b + 1)
    pool.sem_inc(W.passed, 1)
    nc.gpsimd.tensor_scalar(R.got_rstd[:, :], R.got_mean_var[:, :, 1], EPS, None, ALU.add).then_inc(R.got_eps, 1)
    pool.wait_ge(R.got_eps, b + 1)
    nc.gpsimd.tensor_tensor(R.got_rstd[:, :], R.got_rstd[:, :], W.minus_half[:, 0:TT],
                            ALU.pow).then_inc(R.got_rstd_ready, 1)


def collect_load(sp, R, W, b, buf=0, bufs=1):
    if begun(b + 1 - bufs):
        sp.wait_ge(R.x_collected, b + 1 - bufs)
        sp.sem_inc(W.passed, 1)
    sp.dma_start(R.kept[buf][:, :, :], W.kept[b].rearrange("(t p) c -> p t c", p=P)).then_inc(R.kept_loaded[buf], 16)




class Experts:

    def __init__(self, stack, nc, R, events, before):
        F, n = R.width, R.n

        def sb(name, shape, dt=F32):
            return stack.enter_context(nc.sbuf_tensor(f"x{R.layer}_{name}", shape, dt))

        self.w1 = sb("w1", [P, n, F])
        self.tail = sb("tail", [P, n, R.chunks * C + R.chunks + C])
        self.tile_w1 = sb("tile_w1", [P, 2, F])
        self.tile_tail = sb("tile_tail", [P, 4, R.chunks * C + R.chunks + C])
        self.rows = sb("rows", [P, 4, C])
        self.rows_t = sb("rows_t", [P, 2, P])
        self.hidden = sb("hidden", [P, 4, F])
        self.out = sb("out", [P, 4, C])
        (self.weights_loaded, self.turned_full, self.turned_ready, self.up_full, self.w1_ready,
         self.tail_ready) = (events[name] for name in
            "weights_loaded turned_full turned_ready up_full w1_ready tail_ready".split())
        (self.hidden_ready, self.down_full, self.out_ready, self.rows_loaded,
         self.out_written) = (events[name] for name in
            "hidden_ready down_full out_ready rows_loaded out_written".split())
        self.before = before


def tile_events(ctx, nc):
    def sem(name):
        return ctx.enter_context(nc.semaphore("x_" + name))

    names = "weights_loaded turned_full turned_ready up_full w1_ready hidden_ready down_full out_ready"
    events = {name: sem(name) for name in names.split()}
    events["rows_loaded"] = [sem(f"rows_loaded{i}") for i in range(4)]
    events["tail_ready"] = [sem(f"tail_ready{i}") for i in range(2)]
    events["out_written"] = [sem(f"out_written{i}") for i in range(4)]
    return events


def tile_sweep(eng, R, body, ahead):
    lo, hi = 8, R.slots - ahead
    hi -= (hi - lo) % 8
    for s in range(-ahead, lo):
        body(s, s, 0)
    with eng.Fori(0, (hi - lo) // 8) as i:
        for k in range(lo, lo + 8):
            body(i * 8 + k, k, i * 2)
    for s in range(hi, R.slots):
        body(s, s, 0)


def is_slot(R, s):
    return not isinstance(s, int) or 0 <= s < R.slots


def expert_of(eng, R, s):
    return eng.value_load(R.table[0:1, 0, bass.ds(s, 1)], min_val=0, max_val=R.n - 1)


def experts_tensor(pe, nc, R, X, W):
    mm, tr = nc.tensor.matmul, nc.tensor.transpose
    turned = [W.o_ps, W.misc]

    def body(s, k, i4):
        c = s + X.before
        if is_slot(R, s + 2):
            i = (k + 2) % 2
            pe.wait_ge(X.rows_loaded[(k + 2) % 4], 4 * X.before + 16 * (i4 + (k + 2) // 4 + 1))
            if begun(c + 1):
                pe.wait_ge(X.turned_ready, c + 1)
            tr(turned[i][:, 0:P], X.rows[:, (k + 2) % 4, :], W.ident[:, :]).then_inc(X.turned_full, 1)
        if is_slot(R, s + 1):
            i = (k + 1) % 2
            pe.wait_ge(X.w1_ready, c + 2)
            pe.wait_ge(X.turned_ready, c + 2)
            if begun(c):
                pe.wait_ge(X.hidden_ready, c)
            for f in range(R.chunks):
                last = mm(W.s_ps[:, i, f * P:(f + 1) * P], X.tile_w1[:, i, f * P:(f + 1) * P],
                          X.rows_t[:, i, :], start=True, stop=True)
            last.then_inc(X.up_full, 1)
        if is_slot(R, s - 1):
            i = (k - 1) % 2
            pe.wait_ge(X.tail_ready[i], X.before // 2 + i4 * 2 + (k - 1) // 2 + 1)
            pe.wait_ge(X.hidden_ready, c)
            if begun(c - 2):
                pe.wait_ge(X.out_ready, c - 2)
            for f in range(R.chunks):
                last = mm(W.m_ps[:, i, 0:C], X.hidden[:, (k - 1) % 4, f * P:(f + 1) * P],
                          X.tile_tail[:, (k - 1) % 4, f * C:(f + 1) * C],
                          start=(f == 0), stop=(f == R.chunks - 1))
            last.then_inc(X.down_full, 1)

    tile_sweep(pe, R, body, 2)
    body(R.slots, R.slots, 0)


def experts_scalar(act, nc, R, X, W):
    func = ACT.Silu if R.layer == 0 else ACT.Gelu

    def body(s, k, i4):
        c = s + X.before
        if is_slot(R, s + 1):
            i = (k + 1) % 2
            act.wait_ge(X.tail_ready[(k + 1) % 2], X.before // 2 + i4 * 2 + (k + 1) // 2 + 1)
            act.wait_ge(X.up_full, c + 2)
            if begun(c - 2):
                act.wait_ge(X.down_full, c - 2)
            for f in range(R.chunks):
                last = nc.scalar.activation(X.hidden[:, (k + 1) % 4, f * P:(f + 1) * P], W.s_ps[:, i, f * P:(f + 1) * P], func,
                                            bias=X.tile_tail[:, (k + 1) % 4, R.chunks * C + f:R.chunks * C + f + 1])
            last.then_inc(X.hidden_ready, 1)
        if is_slot(R, s + 2) and k % 2 == 1:
            e = expert_of(act, R, s + 2)
            act.wait_ge(X.weights_loaded, R.weights_loads)
            if begun(c - 1):
                act.wait_ge(X.out_ready, c - 1)
                act.sem_inc(W.passed, 1)
            nc.scalar.activation(X.tile_tail[:, (k + 2) % 4, :], X.tail[:, bass.ds(e, 1), :]
                                 .rearrange("p a f -> p (a f)"), ACT.Copy).then_inc(X.tail_ready[k % 2], 1)

        if is_slot(R, s - 2):
            act.wait_ge(X.out_ready, c - 1)
            act.sem_inc(W.passed, 1)
            act.dma_start(W.sorted_out[bass.ds((s - 2) * P, P), :], X.out[:, (k - 2) % 4, :]
                          ).then_inc(X.out_written[(k - 2) % 4], 16)

    tile_sweep(act, R, body, 2)
    for s in range(R.slots, R.slots + 2):
        body(s, s, 0)


def experts_vector(dve, nc, R, X, W):
    v = nc.vector
    turned = [W.o_ps, W.misc]
    dve.wait_ge(X.weights_loaded, R.weights_loads)

    def body(s, k, i4):
        c = s + X.before
        if is_slot(R, s + 2):
            i = (k + 2) % 2
            dve.wait_ge(X.turned_full, c + 3)
            if begun(c + 1):
                dve.wait_ge(X.up_full, c + 1)
            v.tensor_copy(X.rows_t[:, i, :], turned[i][:, 0:P]).then_inc(X.turned_ready, 1)
            if k % 2 == 0:
                e = expert_of(dve, R, s + 2)
                if begun(c - 1):
                    dve.wait_ge(X.out_ready, c - 1)
                v.tensor_copy(X.tile_tail[:, (k + 2) % 4, :], X.tail[:, bass.ds(e, 1), :]
                              .rearrange("p a f -> p (a f)")).then_inc(X.tail_ready[k % 2], 1)
        if is_slot(R, s - 1):
            dve.wait_ge(X.down_full, c)
            if begun(s - 4):
                dve.wait_ge(X.out_written[(k - 1) % 4], 4 * X.before + 16 * (i4 + (k - 1) // 4))
            v.tensor_tensor(X.out[:, (k - 1) % 4, :], W.m_ps[:, (k - 1) % 2, 0:C],
                            X.tile_tail[:, (k - 1) % 4, R.chunks * (C + 1):], ALU.add).then_inc(X.out_ready, 1)

    tile_sweep(dve, R, body, 2)
    body(R.slots, R.slots, 0)


def experts_gpsimd(pool, nc, R, X, W):
    pool.wait_ge(X.weights_loaded, R.weights_loads)

    def body(s, k, i4):
        c = s + X.before
        if is_slot(R, s + 2):
            e = expert_of(pool, R, s + 2)
            if begun(c + 1):
                pool.wait_ge(X.up_full, c + 1)
                pool.sem_inc(W.passed, 1)
            nc.gpsimd.tensor_copy(X.tile_w1[:, (k + 2) % 2, :], X.w1[:, bass.ds(e, 1), :]
                                  .rearrange("p a f -> p (a f)")).then_inc(X.w1_ready, 1)

    tile_sweep(pool, R, body, 2)


AHEAD = 5


def experts_sync(sp, nc, R, X, W):
    def body(s, k, i4):
        c = s + X.before
        if is_slot(R, s + AHEAD):
            row = sp.value_load(R.table[0:1, 1, bass.ds(s + AHEAD, 1)], min_val=0,
                                max_val=R.n * REGION + (R.n - 1) * P)
            if begun(s + AHEAD - 3):
                sp.wait_ge(X.turned_full, c + AHEAD - 3)
                sp.sem_inc(W.passed, 1)
            sp.dma_start(X.rows[:, (k + AHEAD) % 4, :], W.sorted_in[bass.ds(row, P), :]
                         ).then_inc(X.rows_loaded[(k + AHEAD) % 4], 16)

    tile_sweep(sp, R, body, AHEAD)




def table_tensor(pe, nc, R, W):
    mm = nc.tensor.matmul
    E, S = R.n, R.slots
    pe.wait_ge(R.seen_ready, B + 1)
    mm(W.misc[0:E, 0:1], R.seen[:, 0:E], W.ones16[:, 0:1], start=True, stop=True)
    mm(W.misc[:, 8:8 + E], W.ones16[:, :], R.seen[:, 0:E], start=True, stop=True).then_inc(R.counts_full, 1)
    pe.wait_ge(R.tiles_ready, R.layer + 1)
    mm(W.misc[0:E, 64:65], W.upto[0:E, 0:E], R.tiles[0:E, 1:2], start=True, stop=True).then_inc(R.cum_full, 1)
    pe.wait_ge(R.marks_ready, R.layer + 1)
    mm(W.misc[0:1, 128:128 + S], W.ones32[0:E, 0:1], R.marks[0:E, 0:S], start=True, stop=True)
    mm(W.misc[0:1, 320:320 + S], R.tiles[0:E, 1:2], R.marks[0:E, 0:S], start=True, stop=True).then_inc(R.table_full, 1)


def table_vector(dve, nc, R, W):
    v = nc.vector
    E, S = R.n, R.slots
    step = R.table_start
    dve.wait_ge(R.counts_full, R.layer + 1)
    v.tensor_tensor(R.rank[:, 0, 0:E], W.misc[:, 8:8 + E], W.regions[:, 0:E], ALU.add).then_inc(R.table_step, 1)
    dve.wait_ge(R.table_step, step + 1)
    v.tensor_scalar(R.pad_row[:, 0:E], R.rank[:, 0, 0:E], W.partition[:, 0:1], None, ALU.add).then_inc(R.pad_ready, 1)
    v.tensor_scalar(R.gap_i[:, 0, 0:E], W.misc[:, 8:8 + E], float(P - 1), None, ALU.add).then_inc(R.table_step, 1)
    dve.wait_ge(R.table_step, step + 2)
    v.tensor_scalar(R.tiles_i[0:E, 0:1], W.misc[0:E, 0:1], float(P - 1), None, ALU.add).then_inc(R.table_step, 1)
    dve.wait_ge(R.table_step, step + 3)
    v.tensor_scalar(R.tiles_i[0:E, 1:2], R.tiles_i[0:E, 0:1], 7, None, ALU.logical_shift_right).then_inc(R.table_step, 1)
    dve.wait_ge(R.table_step, step + 4)
    v.tensor_copy(R.tiles[0:E, 1:2], R.tiles_i[0:E, 1:2]).then_inc(R.tiles_ready, 1)
    dve.wait_ge(R.cum_full, R.layer + 1)
    v.tensor_copy(R.tiles[0:E, 2:3], W.misc[0:E, 64:65]).then_inc(R.table_step, 1)
    dve.wait_ge(R.table_step, step + 5)
    v.tensor_scalar(R.marks[0:E, 0:S], W.numbers[0:E, 0:S], R.tiles[0:E, 2:3], None, ALU.is_ge).then_inc(R.marks_ready, 1)
    dve.wait_ge(R.table_full, R.layer + 1)
    expert, before = R.table_f[0:1, 0, 0:S], R.table_f[0:1, 1, 0:S]
    v.tensor_copy(expert, W.misc[0:1, 128:128 + S]).then_inc(R.table_step, 1)
    dve.wait_ge(R.table_step, step + 6)
    v.tensor_tensor(before, W.numbers[0:1, 0:S], W.misc[0:1, 320:320 + S], ALU.subtract).then_inc(R.table_step, 1)
    dve.wait_ge(R.table_step, step + 7)
    v.tensor_scalar(before, before, float(P), None, ALU.mult).then_inc(R.table_step, 1)
    dve.wait_ge(R.table_step, step + 8)
    v.scalar_tensor_tensor(before, expert, float(REGION), before, ALU.mult, ALU.add).then_inc(R.table_step, 1)
    dve.wait_ge(R.table_step, step + 9)
    v.tensor_scalar(R.table[0:1, 0, 0:S], expert, float(E - 1), None, ALU.min)
    v.tensor_copy(R.table[0:1, 1, 0:S], before).then_inc(R.table_ready, 1)


def result_rows(dve, nc, R, W):
    v, E = nc.vector, R.n
    step = R.table_start + 9
    gap, rows = R.gap[:, 0:E], R.row_all[:, :, :].rearrange("p t j -> p (t j)")
    v.tensor_scalar(R.gap_i[:, 1, 0:E], R.gap_i[:, 0, 0:E], 7, None, ALU.logical_shift_right).then_inc(R.table_step, 1)
    dve.wait_ge(R.table_step, step + 1)
    v.tensor_copy(gap, R.gap_i[:, 1, 0:E]).then_inc(R.table_step, 1)
    dve.wait_ge(R.table_step, step + 2)
    v.tensor_scalar(gap, gap, -float(P), float(REGION), ALU.mult, ALU.add).then_inc(R.table_step, 1)
    dve.wait_ge(R.table_step, step + 3)
    for e in range(E - 1, 0, -1):
        v.scalar_tensor_tensor(R.shift[:, :], rows, float(e * REGION),
                               R.gap[:, e - 1:e].to_broadcast([P, TILES * TOP]), ALU.is_ge, ALU.mult).then_inc(R.table_step, 1)
        dve.wait_ge(R.table_step, step + 3 + 2 * (E - e) - 1)
        v.tensor_tensor(rows, rows, R.shift[:, :], ALU.subtract).then_inc(R.table_step, 1)
        dve.wait_ge(R.table_step, step + 3 + 2 * (E - e))


def table_gpsimd(pool, nc, R, W):
    pool.wait_ge(R.pad_ready, R.layer + 1)
    for e in range(R.n):
        pool.indirect_dma_start(W.sorted_in, bass.IndirectOffsetOnAxis(ap=R.pad_row[:, e:e + 1], axis=0),
                                W.zeros[:, :], None).then_inc(R.padded, 16)


def table_wait(eng, R, loads=False):
    eng.wait_ge(R.table_ready, R.layer + 1)
    if loads:
        eng.wait_ge(R.scattered, MOVES * B)
        eng.wait_ge(R.padded, 16 * R.n)
        eng.wait_ge(R.zeroed, 16)


def experts_done(eng, R, X):
    for i in range(4):
        eng.wait_ge(X.out_written[i], 4 * X.before + 16 * ((R.slots - i + 3) // 4))


def load_weights(sp, nc, R, X, W):
    w1, b1, w2_dram, b2 = W.experts[R.layer]
    w2, bias1, bias2 = X.tail[:, :, 0:R.chunks * C], X.tail[:, :, R.chunks * C:R.chunks * (C + 1)], X.tail[:, :, R.chunks * (C + 1):]
    sp.dma_start(X.w1[:, :, :], w1.rearrange("e p f -> p e f")).then_inc(X.weights_loaded, 16)
    for e in range(R.n):
        sp.dma_start(w2[:, e, :].rearrange("p (k c) -> p k c", c=C),
                     w2_dram[e].rearrange("(k p) c -> p k c", p=P)).then_inc(X.weights_loaded, 16)
    sp.dma_start(bias1, b1).then_inc(X.weights_loaded, 16)
    sp.dma_start(bias2, b2.partition_broadcast(P)).then_inc(X.weights_loaded, 16)


def final_sweep(eng, body):
    for b in (-1, 0, 1):
        body(b, b, 0)
    with eng.Fori(0, (B - 4) // 2) as i:
        for u in (2, 3):
            body(i * 2 + u, u, i)
    for b in range(B - 2, B + 1):
        body(b, b, 0)


def sandwich(nc, x, consts, weights, out):
    with ExitStack() as ctx:
        def sem(name):
            return ctx.enter_context(nc.semaphore(name))

        class W:
            pass

        loads = []

        def sb(stack, name, shape, dt=F32):
            return stack.enter_context(nc.sbuf_tensor(name + "_sb", shape, dt))

        def constant(name, ap, rows=None):
            if rows is not None:
                ap = ap.partition_broadcast(rows)
            tile = sb(ctx, name, list(ap.shape), ap.dtype)
            loads.append((tile, ap))
            return tile

        x_sb = sb(ctx, "x", [P, TILES, C])
        (W.ident, W.ident16, W.causal, W.before, W.ones16, W.ones32) = (constant(name, consts[name]) for name in
            "ident ident16 causal before ones16 ones32".split())
        (W.zeros, W.upto, W.partition, W.numbers, W.regions, W.minus_half) = (constant(name, consts[name]) for name in
            "zeros upto partition numbers regions minus_half".split())
        W.wq = [constant(f"wq{i}", weights[f"wq{i}"]) for i in range(2)]
        W.wo = [constant(f"wo{i}", weights[f"wo{i}"]) for i in range(2)]
        W.router = [constant(f"router{i}", weights[f"router{i}"]) for i in range(2)]
        (W.wkd, W.wku, W.wk1, W.wv1, W.bq, W.bk) = (constant(name, weights[name]) for name in
            "wkd wku wk1 wv1 bq bk".split())
        (W.bkd, W.mix) = (constant(name, weights[name]) for name in
            "bkd mix".split())
        (W.bv, W.bo, W.g1, W.be1, W.mix_b, W.g2) = (constant(name, weights[name], P) for name in
            "bv bo g1 be1 mix_b g2".split())
        W.be2 = constant("be2", weights["be2"], P)
        W.q_rows, W.k_rows = consts["q_rows"], consts["k_rows"]
        W.experts = weights["experts"]

        def dram(name, shape, dt=F32):
            return nc.dram_tensor(name, shape, dt, kind="Internal").ap()

        W.stack_dram = dram("stack_dram", [2, 64, 2, PAIRS, T], BF16)
        W.max_dram = dram("max_dram", [2, 24, T], BF16)
        W.kept = dram("kept_dram", [B, T, C])
        W.sorted_in = dram("sorted_in", [MAX_E * (REGION + P), C])
        W.sorted_out = dram("sorted_out", [(TOP * TILES + MAX_E) * P, C])

        W.s_ps = ctx.enter_context(nc.psum_tensor("s_ps", [P, 4, T], F32))
        W.m_ps = ctx.enter_context(nc.psum_tensor("m_ps", [P, 2, T], F32))
        W.o_ps = ctx.enter_context(nc.psum_tensor("o_ps", [P, T], F32))
        W.misc = ctx.enter_context(nc.psum_tensor("misc", [P, T], F32))

        constants_loaded, x_first, x_rest, stored = (sem(s) for s in ("constants_loaded", "x_first", "x_rest", "stored"))
        W.passed = sem("passed")
        all_loaded = (constants_loaded, 16 * len(loads))
        bufs = routing_buffers(ctx, nc)
        bufs["passed"] = W.passed
        bufs.update(table_events(ctx, nc))
        tiles = tile_events(ctx, nc)
        R = []
        for layer in range(2):
            experts, _, width = weights["experts"][layer][0].shape
            R.append(Routing(ctx, nc, bufs, layer, experts, width, R[0].table_steps if layer == 1 else 0,
                             R[0].weights_loads if layer == 1 else 0))
        with ExitStack() as stack:
            A = Attention(stack, ctx, nc, x_sb)
        X = []
        for layer in range(2):
            with ExitStack() as stack:
                X.append(Experts(stack, nc, R[layer], tiles, R[0].slots if layer == 1 else 0))
                if layer == 1:
                    last_got = [sb(stack, f"last_got{i}", [P, TT, TOP, C]) for i in range(2)]
                    last_kept = [sb(stack, f"last_kept{i}", [P, TT, C]) for i in range(2)]

        def wait_for_x(eng, layer, b):
            if layer == 1:
                eng.wait_ge(R[0].x_collected, b + 1)
                eng.sem_inc(W.passed, 1)
            elif isinstance(b, int) and b < 2:
                eng.wait_ge(x_first, 16 * 2)
            else:
                eng.wait_ge(x_rest, 16)

        W.wait_for_x = wait_for_x
        x_view = x.rearrange("b (t p) c -> p (b t) c", p=P)
        out_view = out.rearrange("b (t p) c -> p (b t) c", p=P)
        block = ctx.enter_context(nc.Block())

        @block.sync
        def _(sp):
            for b in range(2):
                sp.dma_start(x_sb[:, b * TT:(b + 1) * TT, :], x_view[:, b * TT:(b + 1) * TT, :]).then_inc(x_first, 16)
            for tile, ap in loads[0::2]:
                sp.dma_start(tile[:], ap).then_inc(constants_loaded, 16)
            sp.dma_start(x_sb[:, 2 * TT:, :], x_view[:, 2 * TT:, :]).then_inc(x_rest, 16)
            sp.wait_ge(*all_loaded)
            for layer in range(2):
                attention_sync(sp, nc, A, W, R[layer], R[0], X[layer])
                table_wait(sp, R[layer], True)
                experts_sync(sp, nc, R[layer], X[layer], W)
                experts_done(sp, R[layer], X[layer])

            def body(b, k, i):
                if has(b + 1):
                    collect_load(sp, R[1], W, b + 1, (k + 1) % 2, 2)
                if has(b - 1):
                    sp.wait_ge(R[1].x_collected, b)
                    sp.sem_inc(W.passed, 1)
                    sp.dma_start(out_view[:, bass.ds((b - 1) * TT, TT), :],
                                 x_sb[:, bass.ds((b - 1) * TT, TT), :]).then_inc(stored, 16)

            R[1].kept = last_kept
            final_sweep(sp, body)
            sp.wait_ge(stored, 16 * B)

        @block.tensor
        def _(pe):
            pe.wait_ge(*all_loaded)
            for layer in range(2):
                attention_tensor(pe, nc, A, W, R[layer])
                table_tensor(pe, nc, R[layer], W)
                table_wait(pe, R[layer])
                experts_tensor(pe, nc, R[layer], X[layer], W)

        @block.scalar
        def _(act):
            for tile, ap in loads[1::2]:
                act.dma_start(tile[:], ap).then_inc(constants_loaded, 16)
            act.wait_ge(*all_loaded)
            for layer in range(2):
                attention_scalar(act, nc, A, W, R[layer])
                table_wait(act, R[layer])
                experts_scalar(act, nc, R[layer], X[layer], W)

        @block.vector
        def _(dve):
            dve.wait_ge(*all_loaded)
            R[1].kept = bufs["kept"]
            for layer in range(2):
                if layer == 1:
                    experts_done(dve, R[0], X[0])
                attention_vector(dve, nc, A, W, R[layer], R[0])
                table_vector(dve, nc, R[layer], W)
                table_wait(dve, R[layer])
                result_rows(dve, nc, R[layer], W)
                experts_vector(dve, nc, R[layer], X[layer], W)
            experts_done(dve, R[1], X[1])
            R[1].got, R[1].kept = last_got, last_kept

            def body(b, k, i):
                if isinstance(b, int) and b < 0:
                    collect_index(dve, nc, R[1], 0, 0)
                    collect_index(dve, nc, R[1], 1, 1)
                if has(b):
                    collect_sum(dve, nc, R[1], W, b, k % 2, i + k // 2)
                    if has(b + 2):
                        collect_index(dve, nc, R[1], b + 2, k % 2)
                    collect_add(dve, nc, R[1], A, b, k % 2)

            final_sweep(dve, body)

        @block.gpsimd
        def _(pool):
            pool.wait_ge(*all_loaded)
            for layer in range(2):
                if layer == 1:
                    experts_done(pool, R[0], X[0])
                attention_gpsimd(pool, nc, A, W, R[layer], R[0])
                table_gpsimd(pool, nc, R[layer], W)
                table_wait(pool, R[layer])
                experts_gpsimd(pool, nc, R[layer], X[layer], W)
            experts_done(pool, R[1], X[1])
            R[1].got = last_got

            def body(b, k, i):
                for copy in range(TT * TOP):
                    if has(b + 1):
                        gather(pool, nc, R[1], W, b + 1, (k + 1) % 2, copy, (k + 1) % 2, 2)
                    if has(b) and copy == TT * TOP - 1:
                        collect_rstd(pool, nc, R[1], W, b)

            final_sweep(pool, body)




def heads_apart(a, np):
    a = np.asarray(a)
    lead = a.shape[:-1]
    a = a.reshape(*lead, PAIRS, 2, D)
    return np.ascontiguousarray(np.swapaxes(a, -1, -3).reshape(*lead, C))


def by_partition(b, np):
    b = np.asarray(b)
    return np.ascontiguousarray(b.reshape(b.shape[0], -1, P).transpose(2, 0, 1))


def shape_constants(np, bf16):
    at = np.arange(P)
    q_rows = np.zeros((16, 2, PAIRS, T))
    q_rows[0:3] = 1
    k_rows = np.zeros((2, 16, 2, PAIRS, T))
    k_rows[:, 3:6] = 1
    base = np.float32(2.0 ** (-8.0 / H))
    slopes = np.array([base ** i for i in range(1, H + 1)], np.float32).astype(np.float64)
    for half in range(2):
        bias = slopes[half::2][:, None] * np.arange(T)[None, :] / SCALE
        for part in range(3):
            k_rows[1, part, half] = bias.astype(bf16).astype(np.float64)
            bias = bias - k_rows[1, part, half]
    f = np.float32
    slots = TOP * TILES + MAX_E
    return dict(
        ident=np.eye(P, dtype=f), ident16=np.eye(P).astype(bf16),
        causal=np.where(at[None, :] > at[:, None], NEG, 0.0).astype(bf16),
        before=(at[:, None] < at[None, :]).astype(bf16), ones16=np.ones((P, P)).astype(bf16),
        ones32=np.ones((P, 2), f), zeros=np.zeros((P, C), f),
        upto=(np.arange(MAX_E)[:, None] <= np.arange(MAX_E)[None, :]).astype(f),
        partition=at[:, None].astype(f), numbers=np.tile(np.arange(slots, dtype=f), (P, 1)),
        regions=np.tile(np.arange(MAX_E, dtype=f) * REGION, (P, 1)), minus_half=np.full((P, 8), -0.5, f),
        q_rows=q_rows.astype(bf16), k_rows=k_rows.astype(bf16),
    )


def kernel(L0_attn_x, L0_attn_Wq, L0_attn_bq, L0_attn_Wkd, L0_attn_bkd, L0_attn_Wku, L0_attn_bku, L0_attn_Wo,
           L0_attn_bo, L0_ffn_g1, L0_ffn_be1, L0_ffn_mix_w, L0_ffn_mix_b, L0_ffn_g2, L0_ffn_be2, L0_ffn_router_w,
           L0_ffn_w1, L0_ffn_b1, L0_ffn_w2, L0_ffn_b2, L1_attn_Wq, L1_attn_Wk, L1_attn_Wv, L1_attn_Wo,
           L1_ffn_gate_w, L1_ffn_w1, L1_ffn_b1, L1_ffn_w2, L1_ffn_b2):
    import ml_dtypes
    import numpy as np
    import concourse.bacc as bacc
    from concourse.bass_utils import run_bass_kernel_spmd

    def a(v):
        return np.ascontiguousarray(np.asarray(v))

    wku, bku = a(L0_attn_Wku), a(L0_attn_bku)
    wku = np.concatenate([heads_apart(wku[:, :C], np), wku[:, C:]], axis=1)
    named = dict(
        wq0=heads_apart(L0_attn_Wq, np), wq1=heads_apart(a(L1_attn_Wq).T, np),
        wo0=a(L0_attn_Wo), wo1=a(a(L1_attn_Wo).T), router0=a(L0_ffn_router_w), router1=a(a(L1_ffn_gate_w).T),
        wkd=a(L0_attn_Wkd), wku=a(np.concatenate([wku, wku], axis=0)),
        wk1=heads_apart(a(L1_attn_Wk).T, np), wv1=a(a(L1_attn_Wv).T),
        bq=heads_apart(L0_attn_bq, np)[:, None], bk=heads_apart(bku[:C], np)[:, None], bkd=a(L0_attn_bkd)[:, None],
        mix=a(L0_ffn_mix_w), bv=a(bku[C:]), bo=a(L0_attn_bo), g1=a(L0_ffn_g1), be1=a(L0_ffn_be1),
        mix_b=a(L0_ffn_mix_b), g2=a(L0_ffn_g2), be2=a(L0_ffn_be2),
        e0_w1=a(L0_ffn_w1), e0_b1=by_partition(L0_ffn_b1, np), e0_w2=a(L0_ffn_w2), e0_b2=a(L0_ffn_b2),
        e1_w1=a(L1_ffn_w1), e1_b1=by_partition(L1_ffn_b1, np), e1_w2=a(L1_ffn_w2), e1_b2=a(L1_ffn_b2),
    )
    constants = shape_constants(np, ml_dtypes.bfloat16)
    arrays = {"x": a(L0_attn_x), **named, **constants}
    arrays = {name: a(v) for name, v in arrays.items()}
    nc = bacc.Bacc("TRN2", target_bir_lowering=False, num_devices=1)
    aps = {name: nc.dram_tensor("in_" + name, v.shape, mybir.dt.from_np(v.dtype), kind="ExternalInput").ap()
           for name, v in arrays.items()}
    out = nc.dram_tensor("out", (B, T, C), F32, kind="ExternalOutput").ap()
    weights = {name: aps[name] for name in named if name[:3] not in ("e0_", "e1_")}
    weights["experts"] = [[aps[f"e{layer}_{w}"] for w in ("w1", "b1", "w2", "b2")] for layer in range(2)]
    sandwich(nc, aps["x"], {name: aps[name] for name in constants}, weights, out)
    result = run_bass_kernel_spmd(nc, [{"in_" + name: v for name, v in arrays.items()}], core_ids=[0])
    return result.results[0]["out"]
```
